# Optimizing a Trainium2 kernel written in Bass

```python
import numpy as np
import jax
import jax.numpy as jnp

def _softmax(x, axis=-1):
    return jax.nn.softmax(x, axis=axis)

def _gelu(x):
    return jax.nn.gelu(x, approximate=True)

def _silu(x):
    return jax.nn.silu(x)

def _sigmoid(x):
    return jax.nn.sigmoid(x)

def _layernorm(x, axis=-1, eps=1e-05):
    m = jnp.mean(x, axis=axis, keepdims=True)
    v = jnp.var(x, axis=axis, keepdims=True)
    return (x - m) / jnp.sqrt(v + eps)

def _scatter_add(tgt, idx, src, axis=0):
    return tgt.at[idx].add(src)

def _segment_sum(src, seg, n):
    return jax.ops.segment_sum(src, seg, n)
kernel_name = 'mk_macaron_d1_jaxref_r4_939477'

def setup_inputs(seed: int=0):
    np.random.seed(seed)
    _w = jnp.asarray

    def _L0_attn_setup():
        import jax, jax.numpy as jnp
        import numpy as np
        B, N, D, H = (2, 512, 256, 8)
        DH = D // H
        key = jax.random.key(seed)
        k0, k1, k2 = jax.random.split(key, 3)
        s = 1.0 / np.sqrt(D).astype(np.float32)
        return {'x': jax.random.normal(k0, (B, N, D), dtype=jnp.float32), 'w_qkv': jax.random.normal(k1, (3 * D, D), dtype=jnp.float32) * s, 'b_qkv': jnp.zeros((3 * D,), dtype=jnp.float32), 'w_o': jax.random.normal(k2, (D, D), dtype=jnp.float32) * s, 'b_o': jnp.zeros((D,), dtype=jnp.float32)}
    _L0_attn_in = _L0_attn_setup()

    def _L0_ffn_setup():
        import jax, jax.numpy as jnp
        import numpy as np
        from functools import partial
        HEADS = 16
        EPS = 1e-12

        def _l2_normalize(z):
            n = jnp.linalg.norm(z, axis=-1, keepdims=True)
            return z / jnp.maximum(n, EPS)
        key = jax.random.key(seed)
        kx, kq, kk, kv, ko, kf = jax.random.split(key, 6)
        B, S, D, L = (2, 512, 256, 256)
        scale = 0.02
        return {'x': jax.random.normal(kx, (B, S, D), dtype=jnp.float32), 'Wq': jax.random.normal(kq, (D, L), dtype=jnp.float32) * scale, 'Wk': jax.random.normal(kk, (D, L), dtype=jnp.float32) * scale, 'Wv': jax.random.normal(kv, (D, L), dtype=jnp.float32) * scale, 'Wo': jax.random.normal(ko, (L, D), dtype=jnp.float32) * scale, 'Wff': jax.random.normal(kf, (D, D), dtype=jnp.float32) * scale}
    _L0_ffn_in = _L0_ffn_setup()
    _d = {'L0_attn_x': _L0_attn_in['x'], 'L0_attn_w_qkv': _L0_attn_in['w_qkv'], 'L0_attn_b_qkv': _L0_attn_in['b_qkv'], 'L0_attn_w_o': _L0_attn_in['w_o'], 'L0_attn_b_o': _L0_attn_in['b_o'], 'L0_ffn_Wq': _L0_ffn_in['Wq'], 'L0_ffn_Wk': _L0_ffn_in['Wk'], 'L0_ffn_Wv': _L0_ffn_in['Wv'], 'L0_ffn_Wo': _L0_ffn_in['Wo'], 'L0_ffn_Wff': _L0_ffn_in['Wff']}
    _x0 = _d['L0_attn_x']
    _d['L0_attn_x'] = jax.random.normal(jax.random.fold_in(jax.random.key(seed), 1), (8, 1024, 256), dtype=_x0.dtype)
    del _x0
    return _d

def reference(L0_attn_x, L0_attn_w_qkv, L0_attn_b_qkv, L0_attn_w_o, L0_attn_b_o, L0_ffn_Wq, L0_ffn_Wk, L0_ffn_Wv, L0_ffn_Wo, L0_ffn_Wff):

    def _L0_attn_ref(x, w_qkv, b_qkv, w_o, b_o):
        import jax, jax.numpy as jnp
        import numpy as np
        B, N, D, H = (2, 512, 256, 8)
        DH = D // H
        b, n, d = x.shape
        h = H
        dh = d // h
        qkv = x @ w_qkv.T + b_qkv
        qkv = qkv.reshape(b, n, 3, dh, h)
        qkv = jnp.transpose(qkv, (2, 0, 4, 1, 3))
        q, k, v = (qkv[0], qkv[1], qkv[2])
        attn = jnp.einsum('bhik,bhjk->bhij', q, k)
        out = jnp.einsum('bhik,bhkj->bhij', attn, v)
        out = jnp.transpose(out, (0, 2, 1, 3)).reshape(b, n, d)
        return out @ w_o.T + b_o

    def _L0_ffn_ref(x, Wq, Wk, Wv, Wo, Wff):
        import jax, jax.numpy as jnp
        import numpy as np
        from functools import partial
        HEADS = 16
        EPS = 1e-12

        def _l2_normalize(z):
            n = jnp.linalg.norm(z, axis=-1, keepdims=True)
            return z / jnp.maximum(n, EPS)
        B, S, D = x.shape
        H = HEADS
        L = Wq.shape[1]
        dh = L // H

        def split_heads(t):
            return t.reshape(B, S, H, dh).transpose(0, 2, 1, 3).reshape(B * H, S, dh)
        q = split_heads(x @ Wq)
        k = split_heads(x @ Wk)
        v = split_heads(x @ Wv)
        scores = jnp.einsum('bqd,bkd->bkq', q, k) / jnp.sqrt(jnp.asarray(D, x.dtype))
        attn = jax.nn.softmax(scores, axis=-1)
        out = jnp.einsum('bkq,bkv->bqv', attn, v)
        z = out.reshape(B, H, S, dh).transpose(0, 2, 1, 3).reshape(B, S, L)
        z = z @ Wo
        z = _l2_normalize(z)
        z = z @ Wff
        z = _l2_normalize(z)
        z = jax.nn.gelu(z, approximate=False)
        return z
    x = L0_attn_x
    x = x + 0.5 * _L0_ffn_ref(_layernorm(x, axis=-1), L0_ffn_Wq, L0_ffn_Wk, L0_ffn_Wv, L0_ffn_Wo, L0_ffn_Wff)
    x = x + _L0_attn_ref(_layernorm(x, axis=-1), L0_attn_w_qkv, L0_attn_b_qkv, L0_attn_w_o, L0_attn_b_o)
    x = x + 0.5 * _L0_ffn_ref(_layernorm(x, axis=-1), L0_ffn_Wq, L0_ffn_Wk, L0_ffn_Wv, L0_ffn_Wo, L0_ffn_Wff)
    return x

_drawn_inputs = setup_inputs


def setup_inputs(seed=0):
    import zlib

    import numpy as np

    out = dict(_drawn_inputs(seed))
    spreads = {'L0_attn_b_qkv': (0.0, 0.1), 'L0_attn_b_o': (0.0, 0.8)}
    factors = {'L0_ffn_Wq': 8.0, 'L0_ffn_Wk': 8.0}
    for name, (base, spread) in spreads.items():
        noise = np.random.default_rng([zlib.crc32(name.encode()), seed]).standard_normal(out[name].shape)
        drawn = base * np.exp(spread * noise) if base else spread * noise
        out[name] = jnp.asarray(drawn.astype(out[name].dtype))
    for name, factor in factors.items():
        out[name] = (out[name] * factor).astype(out[name].dtype)
    return out
```

```python
import concourse.bass as bass
from concourse import mybir
from contextlib import ExitStack


def build_macaron(nc, x_in, w_qkv, b_qkv, w_o, b_o, Wq, Wk, Wv, Wo, Wff, out):
    f32, bf16 = mybir.dt.float32, mybir.dt.bfloat16
    ALU, ACT, AX = mybir.AluOpType, mybir.ActivationFunctionType, mybir.AxisListType

    B, N, D = x_in.shape
    P = 128
    DC = D // P
    NT = N // P
    BANK = 512
    NB = N // BANK
    FH, FD = 16, D // 16
    AH = 8
    QUARTERS = 4
    HQ = FH // QUARTERS
    TILES = FH * NT
    GROUPS = TILES // HQ
    QT = TILES // QUARTERS
    QG = GROUPS // QUARTERS
    HALVES = 2
    EG = 3
    NM = 8
    SLOTS = 3
    PHASES = 2 * B
    LINEAR = B + 1
    LN_EPS, NORM_EPS2 = 1e-5, 1e-24
    SCORE_SCALE = float(D) ** -0.5
    TERMS = [(0, 0), (0, 1), (1, 0), (1, 1), (0, 2), (2, 0), (1, 2), (2, 1)]
    STACK = 16 * len(TERMS) * HQ
    assert len(TERMS) * FD == P

    xs = nc.dram_tensor("x_slots", (3 * B, N, D), f32, kind="Internal").ap()

    def tokens(rows):
        return rows.rearrange("(t p) d -> p t d", p=P)

    def phase_steps(tiles, prep, post, linear):
        at = {}

        def put(tile, *step):
            at.setdefault(tile, []).append(step)

        if post:
            for t in range(NT):
                put(2 + 3 * t, "u", t)
            put(26, "u_floor")
            put(26, "u_norm")
            put(29, "w_floor")
            put(29, "w_norm")
            put(33, "gelu")
            for k in range(2):
                put(35 + 2 * k, "x1", k)
            if linear:
                for t in range(NT):
                    put(37 + t, "ln2_stats", t)
                put(46, "ln2_aggr")
                put(47, "ln2_rstd")
                for t in range(NT):
                    put(50 + t, "xn2", t)
                put(60, "gram", 0)
                put(64, "gram", 1)
                put(67, "xt2", 0)
                put(70, "T")
                put(73, "xt2", 1)
                put(77, "VK")
                put(84, "G")
                put(91, "H")
                for k in range(4):
                    put(94 + k, "xbias", k)
                for k in range(4):
                    put(100 + 3 * k, "y", k)
        if prep:
            for t in range(NT):
                put(6 + 2 * t, "ln_stats", t)
            put(22, "ln_aggr")
            put(23, "ln_rstd")
            for t in range(NT):
                put(26 + t, "xn", t)
            for dh in range(DC):
                put(36 + 3 * dh, "xt", dh)
            for i in range(4):
                put(42 + 3 * i, "qk", i)
            for k in range(4):
                put(54 + 3 * k, "v", k)
            for i in range(4, 8):
                put(112 + 3 * (i - 4), "qk", i)
        if not tiles:
            order = []
            for t in sorted(at):
                order += at[t]
            if prep:
                order.sort(key=lambda s: s[0] == "v")
            return order
        order = [("v_swap",)]
        for t in range(TILES):
            order += at.get(t, [])
            order.append(("tile", t))
            if t % HQ == 1 and t > HQ:
                order.append(("recip", t // HQ - 1))
            if t % HQ == 1 and t >= 2 * HQ:
                order.append(("av", t // HQ - 2, 0))
            if t % HQ == 3 and t >= 2 * HQ:
                order.append(("av", t // HQ - 2, 1))
            if t == TILES // 2 + 7:
                order.append(("z", 0))
        order.append(("recip", GROUPS - 1))
        for g in (GROUPS - 2, GROUPS - 1):
            for n in range(NB):
                order.append(("av", g, n))
        order.append(("z", 1))
        return order

    PSUM_STEPS = {"tile", "u", "gram", "xt2", "T", "VK", "G", "H", "y", "xt", "qk", "v"}
    PER = {"tile": TILES, "u": NT, "gram": DC, "xt2": DC, "T": 1, "VK": 1, "G": 1, "H": 1, "y": 4,
           "xt": DC, "qk": 8, "v": 4}

    prologue = phase_steps(False, True, False, False)
    linear_body = phase_steps(True, True, True, True)
    plain_body = phase_steps(True, True, True, False)
    epilogue = phase_steps(False, False, True, False)

    ctx = ExitStack()
    with ctx:
        def sb(name, shape, dt=f32):
            return ctx.enter_context(nc.sbuf_tensor(name, shape, dt))

        def sem(name):
            return ctx.enter_context(nc.semaphore(name))

        wqkv = sb("ffn_wqkv", [P, DC, 3 * D])
        wow = sb("ffn_wo_wowff", [P, DC, 2 * D])
        wkv = sb("attn_wkv", [P, DC, 2 * D])
        wqn = sb("attn_wq_rows", [P, DC, D])
        wop = sb("attn_wo_cols", [P, DC, D])
        brow = sb("attn_bkv_row", [1, 2 * D])
        nbrow = sb("attn_nbv_row", [1, 2 * D])
        bqc = sb("attn_bq_col", [P, DC])
        bqb = sb("attn_bq_wide", [P, DC, P])
        bob = sb("attn_bo_wide", [P, D])
        ident = sb("identity", [P, P])
        mask = sb("head_mask", [P, AH])
        half_neg = sb("minus_half", [P, NT])
        zero = sb("zero", [P, 1])
        E = sb("exp_ring", [P, EG * HQ, N])
        stack = [sb(f"kq_stack{i}", [P, 2, HQ, N], bf16) for i in range(2)]
        parts = [sb(f"kq_parts{h}", [P, 6, N], bf16) for h in range(HALVES)]
        qstage = sb("kq_stage", [P, 2, BANK])
        resid = sb("kq_rest", [P, BANK])
        vnext = sb("v_next", [P, NT, D])
        vcur = sb("v_now", [P, NT, D])
        vsc = [sb(f"v_scaled{a}", [P, EG, HQ, 2 * FD]) for a in range(2)]
        negmax = sb("neg_max", [P, NM])
        sums = sb("exp_sums", [P, EG, HQ])
        rsum = sb("exp_rsums", [P, EG, HQ])
        zT = sb("o_T", [P, HALVES, N])
        xp = sb("x_prep", [P, NT, D])
        xr = sb("x_post", [P, NT, D])
        XT = sb("xn_T", [P, DC, N])
        XT2 = xp[:].rearrange("p (c t) d -> p c (t d)", c=DC)
        wb = sb("w_xn2", [P, NT, D + 1])
        stats = sb("bn_stats", [P, NT, 6])
        mv = sb("bn_mv", [P, NT, 2])
        rstd = sb("rstd", [P, NT])
        stats2 = sb("bn_stats2", [P, NT, 6])
        mv2 = sb("bn_mv2", [P, NT, 2])
        rstd2 = sb("rstd2", [P, NT])
        ssu = sb("sumsq_u", [P, NT])
        ssw = sb("sumsq_w", [P, NT])
        unorm = sb("u_rnorm", [P, NT])
        sink = sb("wait_sink", [P, 1])
        gsc = sb("gelu_scale", [P, NT])
        S = sb("gram_then_vk", [P, DC, D + 1])
        VK = S
        T = sb("t_then_g", [P, DC, D])
        G = T
        H = sb("h", [P, DC, D])
        rrow = sb("r_row", [1, 2 * D])
        biasw = sb("bias_wide", [P, D])

        ring = ctx.enter_context(nc.psum_tensor("ring", [P, SLOTS, NB, BANK], f32))
        O = ctx.enter_context(nc.psum_tensor("o_acc", [P, NB, BANK], f32))

        tmp = E[:, 0, :].rearrange("p (a n) -> p a n", a=4)
        wo_T, wff_sb = tmp[:, 0:2, :], tmp[:, 2:4, :]
        kv_rows = E[:, 1, :].rearrange("p (a n) -> p a n", a=4)
        wo_rows = E[:, 2, 0:2 * D].rearrange("p (a n) -> p a n", a=2)
        wo_perm = E[:, 2, 2 * D:4 * D].rearrange("p (a n) -> p a n", a=2)

        w_loaded = sem("w_loaded")
        x_copied = sem("x_copied")
        xp_loaded = sem("xp_loaded")
        xr_loaded = sem("xr_loaded")
        x_stored = sem("x_stored")
        out_stored = sem("out_stored")
        stacked = [sem(f"stacked{i}") for i in range(2)]
        const_ready = sem("const_ready")
        const_dve = sem("const_dve")
        setup_pe = sem("setup_pe")
        setup_act = sem("setup_act")
        filled = {k: sem(f"filled_{k}") for k in sorted(PSUM_STEPS)}
        max_ready = sem("max_ready")
        exp_done = sem("exp_done")
        rsum_ready = sem("rsum_ready")
        vsc_ready = sem("vsc_ready")
        av_done = sem("av_done")
        v_swapped = sem("v_swapped")
        z_act = sem("z_act")
        u_act = sem("u_act")
        w_sq = sem("w_sq")
        w_dve = sem("w_dve")
        u_floored = sem("u_floored")
        w_floored = sem("w_floored")
        norm_step = sem("norm_step")
        var_ready = sem("var_ready")
        var2_ready = sem("var2_ready")
        gelu_done = sem("gelu_done")
        x1_done = sem("x1_done")
        ln_stats = sem("ln_stats")
        ln_aggr = sem("ln_aggr")
        rstd_ready = sem("rstd_ready")
        xn_ready = sem("xn_ready")
        xt_act = sem("xt_act")
        qk_act = sem("qk_act")
        split_step = sem("split_step")
        v_act = sem("v_act")
        ln2_stats = sem("ln2_stats")
        ln2_aggr = sem("ln2_aggr")
        rstd2_ready = sem("rstd2_ready")
        xn2_ready = sem("xn2_ready")
        xt2_act = sem("xt2_act")
        gram_act = sem("gram_act")
        T_act = sem("T_act")
        VK_dve = sem("VK_dve")
        G_act = sem("G_act")
        H_act = sem("H_act")
        bias_dve = sem("bias_dve")
        xbias_done = sem("xbias_done")
        y_dve = sem("y_dve")

        FREED = {"tile": [exp_done], "u": [w_sq], "gram": [gram_act], "xt2": [xt2_act],
                 "T": [T_act], "VK": [VK_dve], "G": [G_act], "H": [H_act, bias_dve],
                 "y": [y_dve], "xt": [xt_act], "qk": [qk_act], "v": [v_act]}
        START = 1
        COUNT_FROM_START = [*filled.values(), *dict.fromkeys(s for k in FREED for s in FREED[k]),
                            x_stored, out_stored, av_done, z_act, vsc_ready, xbias_done]
        PREP = {"xt", "qk", "v"}

        def index(step):
            return step[1] if len(step) > 1 else 0

        def before(p, kind):
            return (p + 1) * PER[kind] if kind in PREP else p * PER[kind]

        def slots_of(steps):
            found, n, had = {}, 0, {}
            for s in steps:
                if s[0] in PSUM_STEPS:
                    found[s] = (n % SLOTS, had.get(n % SLOTS))
                    had[n % SLOTS] = s
                    n += 1
            return found

        def sections(engine, part):
            part(prologue, -1, True)
            with engine.Fori(0, LINEAR) as p:
                part(linear_body, p, True)
            with engine.Fori(LINEAR, PHASES) as p:
                part(plain_body, p, False)
            part(epilogue, PHASES, False)

        block = ctx.enter_context(nc.Block())

        @block.sync
        def _(sp):
            for s in COUNT_FROM_START:
                sp.sem_inc(s, START)
            sp.dma_start(xp[:], tokens(x_in[0])).then_inc(xp_loaded, 16)
            for i, w in enumerate((Wq, Wk, Wv)):
                sp.dma_start(wqkv[:, :, i * D:(i + 1) * D],
                             w.rearrange("(c p) n -> p c n", p=P)).then_inc(w_loaded, 16)
            sp.dma_start(wow[:, :, 0:D], Wo.rearrange("(c p) n -> p c n", p=P)).then_inc(w_loaded, 16)
            sp.dma_start(wff_sb, Wff.rearrange("(c p) n -> p c n", p=P)).then_inc(w_loaded, 16)
            sp.dma_start(wqn[:], w_qkv[0:D].rearrange("(c p) n -> p c n", p=P)).then_inc(w_loaded, 16)
            sp.dma_start(kv_rows, w_qkv[D:3 * D].rearrange("(c p) n -> p c n", p=P)).then_inc(w_loaded, 16)
            sp.dma_start(wo_rows, w_o.rearrange("(c p) n -> p c n", p=P)).then_inc(w_loaded, 16)
            sp.dma_start(brow[:], b_qkv[D:3 * D].rearrange("(a n) -> a n", a=1)).then_inc(w_loaded, 16)
            sp.dma_start(bqc[:], b_qkv[0:D].rearrange("(c p) -> p c", p=P), allow_slow_non_contiguous=True).then_inc(w_loaded, 16)
            sp.dma_start(bob[:], b_o.rearrange("(a n) -> a n", a=1).to_broadcast([P, D])).then_inc(w_loaded, 16)
            sp.dma_start(xs[PHASES - 1], x_in[0]).then_inc(x_copied, 16)
            sp.dma_start(xs[0:B], x_in).then_inc(x_copied, 16)

            def stack_quarter(q, split=None):
                half, a = q // 2, q % 2
                for t, (kp, qp) in enumerate(TERMS):
                    for c in range(HQ):
                        rows = FD * (2 * c + a)
                        if split is not None and (t, c) == (len(TERMS) - 1, HQ - 1):
                            sp.wait_ge(split_step, split)
                        sp.dma_start(stack[q % 2][FD * t:FD * (t + 1), :, c, :],
                                     parts[half][rows:rows + FD, kp:qp + 4:3 + qp - kp, :]
                                     ).then_inc(stacked[q % 2], 16)

            sp.wait_ge(split_step, 16)
            stack_quarter(0)

            def phase(p, linear):
                if linear:
                    sp.wait_ge(x_stored, START + p * 16)
                    sp.wait_ge(x_copied, 32)
                    sp.dma_start(xr[:], tokens(xs[(p + PHASES - 1) % PHASES])).then_inc(xr_loaded, 16)
                else:
                    sp.wait_ge(x_stored, START + LINEAR * 16)
                    sp.wait_ge(out_stored, START + (p - LINEAR) * 16)
                    sp.dma_start(xr[:], tokens(xs[p - 1])).then_inc(xr_loaded, 16)
                sp.wait_ge(filled["y"], START + (p if linear else LINEAR) * 4)
                sp.wait_ge(filled["xt"], START + (p + 1) * DC)
                sp.dma_start(xp[:], tokens(xs[(p + 1) % PHASES])).then_inc(xp_loaded, 16)
                for q in (1, 2, 3):
                    sp.wait_ge(filled["tile"], START + p * TILES + QT * (q - 1))
                    stack_quarter(q, {1: (p + 1) * 32, 3: (p + 1) * 32 + 16}.get(q))
                sp.wait_ge(filled["tile"], START + p * TILES + QT * (QUARTERS - 1))
                stack_quarter(0)
                if linear:
                    sp.wait_ge(y_dve, START + (p + 1) * 4)
                    sp.dma_start(tokens(xs[(p + PHASES - 1) % PHASES + B]), xr[:]).then_inc(x_stored, 16)
                else:
                    sp.wait_ge(x1_done, (p + 1) * 2)
                    sp.dma_start(tokens(out[p - LINEAR]), xr[:]).then_inc(out_stored, 16)

            sp.wait_ge(x_copied, 32)
            with sp.Fori(0, LINEAR) as p:
                phase(p, True)
            with sp.Fori(LINEAR, PHASES) as p:
                phase(p, False)
            sp.wait_ge(out_stored, START + (B - 1) * 16)
            sp.dma_start(xr[:], tokens(xs[PHASES - 1])).then_inc(xr_loaded, 16)
            sp.wait_ge(x1_done, (PHASES + 1) * 2)
            sp.dma_start(tokens(out[B - 1]), xr[:]).then_inc(out_stored, 16)
            sp.wait_ge(out_stored, START + B * 16)
            sp.wait_ge(stacked[0], (2 * PHASES + 1) * STACK)
            sp.wait_ge(xp_loaded, (PHASES + 1) * 16)

        @block.gpsimd
        def _(pool):
            nc.gpsimd.memset(ident[:], 0.0).then_inc(const_ready, 1)
            pool.wait_ge(const_ready, 1)
            nc.gpsimd.affine_select(out=ident[:], in_=ident[:], compare_op=ALU.not_equal, fill=1.0,
                                    base=0, pattern=[[-1, P]], channel_multiplier=1).then_inc(const_ready, 1)
            nc.gpsimd.memset(half_neg[:], -0.5).then_inc(const_ready, 1)
            nc.gpsimd.memset(zero[:], 0.0).then_inc(const_ready, 1)
            for a in range(2):
                nc.gpsimd.memset(vsc[a][:], 0.0).then_inc(const_ready, 1)
            pool.wait_ge(const_ready, 6)

            def part(steps, p, linear):
                for step in steps:
                    kind, i = step[0], index(step)
                    if kind == "ln_rstd":
                        pool.wait_ge(var_ready, p + 2)
                        nc.gpsimd.tensor_tensor(rstd[:], rstd[:], half_neg[:], ALU.pow).then_inc(rstd_ready, 1)
                    elif kind == "ln2_rstd":
                        pool.wait_ge(var2_ready, p + 1)
                        nc.gpsimd.tensor_tensor(rstd2[:], rstd2[:], half_neg[:], ALU.pow).then_inc(rstd2_ready, 1)
                    elif kind == "qk":
                        half, m, n = i // 4, (i // 2) % 2, i % 2
                        piece, rest = qstage[:, i % 2, :], resid[:]
                        zeros = zero[:, 0:1].to_broadcast([P, BANK])

                        def to(k):
                            return parts[half][:, 3 * m + k, n * BANK:(n + 1) * BANK]

                        at = (p + 1) * 32 + i * 4
                        pool.wait_ge(qk_act, START + (p + 1) * PER["qk"] + i + 1)
                        if i % 4 == 0 and not isinstance(p, int):
                            for s in stacked:
                                pool.wait_ge(s, p * 2 * STACK + (half + 1) * STACK)
                        nc.gpsimd.tensor_tensor(to(0), piece, zeros, ALU.add).then_inc(split_step, 1)
                        pool.wait_ge(split_step, at + 1)
                        nc.gpsimd.tensor_tensor(rest, piece, to(0), ALU.subtract).then_inc(split_step, 1)
                        pool.wait_ge(split_step, at + 2)
                        nc.gpsimd.tensor_tensor(to(1), rest, zeros, ALU.add).then_inc(split_step, 1)
                        pool.wait_ge(split_step, at + 3)
                        nc.gpsimd.tensor_tensor(to(2), rest, to(1), ALU.subtract).then_inc(split_step, 1)
                        pool.wait_ge(split_step, at + 4)
                    elif kind == "recip":
                        g = i
                        q, j = g // QG, g % QG
                        half, a = q // 2, q % 2
                        pool.wait_ge(v_swapped, p + 1)
                        pool.wait_ge(rsum_ready, p * GROUPS + g + 1)
                        if g >= EG:
                            pool.wait_ge(av_done, START + p * GROUPS + g - EG + 1)
                        else:
                            pool.wait_ge(av_done, START + p * GROUPS)
                        heads = vcur[:, j, half * P:(half + 1) * P].rearrange(
                            "p (c a d) -> p c a d", c=HQ, a=2)[:, :, a, :]
                        nc.gpsimd.tensor_tensor(
                            vsc[a][:, g % EG, :, a * FD:(a + 1) * FD], heads,
                            rsum[:, g % EG, :].unsqueeze(2).to_broadcast([P, HQ, FD]),
                            ALU.mult).then_inc(vsc_ready, 1)
                    elif kind == "u_norm":
                        a = unorm[:]
                        pool.wait_ge(u_floored, p + 1)
                        nc.gpsimd.tensor_tensor(a, ssu[:], half_neg[:], ALU.pow).then_inc(norm_step, 1)
                        pool.wait_ge(w_sq, START + (p + 1) * NT)
                        pool.wait_ge(norm_step, p * 5 + 1)
                        nc.gpsimd.tensor_tensor(ssw[:], ssw[:], a, ALU.mult).then_inc(norm_step, 1)
                        pool.wait_ge(norm_step, p * 5 + 2)
                        nc.gpsimd.tensor_tensor(ssw[:], ssw[:], a, ALU.mult).then_inc(norm_step, 1)
                    elif kind == "w_norm":
                        pool.wait_ge(w_floored, p + 1)
                        nc.gpsimd.tensor_tensor(ssw[:], ssw[:], half_neg[:], ALU.pow).then_inc(norm_step, 1)
                        pool.wait_ge(norm_step, p * 5 + 4)
                        nc.gpsimd.tensor_tensor(gsc[:], ssw[:], unorm[:], ALU.mult).then_inc(norm_step, 1)
                    elif kind == "xbias":
                        pool.wait_ge(bias_dve, START + p + 1)
                        pool.wait_ge(x1_done, (p + 1) * 2)
                        nc.gpsimd.tensor_tensor(
                            xr[:, 2 * i:2 * i + 2, :], xr[:, 2 * i:2 * i + 2, :],
                            biasw[:].unsqueeze(1).to_broadcast([P, 2, D]), ALU.add).then_inc(xbias_done, 1)

            sections(pool, part)

        @block.scalar
        def _(act):
            act.wait_ge(setup_pe, 1)
            nc.scalar.copy(wo_T, ring[:, 0, 0, :].rearrange("p (a n) -> p a n", a=2)).then_inc(setup_act, 1)
            act.wait_ge(setup_pe, 2)
            nc.scalar.copy(wkv[:], ring[:, 1, :, :]).then_inc(setup_act, 1)
            act.wait_ge(setup_pe, 3)
            nc.scalar.copy(wop[:], ring[:, 2, 0, :].rearrange("p (a n) -> p a n", a=2)).then_inc(setup_act, 1)
            act.wait_ge(setup_pe, 4)
            nc.scalar.copy(wow[:, :, D:2 * D],
                           ring[:, 0, 0, :].rearrange("p (a n) -> p a n", a=2)).then_inc(setup_act, 1)

            def part(steps, p, linear):
                slot = slots_of(steps)
                for step in steps:
                    kind, i = step[0], index(step)
                    if kind in filled and kind != "y" and kind != "VK":
                        act.wait_ge(filled[kind], START + before(p, kind) + i + 1)
                        ps = ring[:, slot[step][0], :, :]
                    if kind == "tile":
                        g, c = i // HQ, i % HQ
                        act.wait_ge(max_ready, p * TILES + i + 1)
                        if c == 0:
                            if g >= EG:
                                act.wait_ge(av_done, START + p * GROUPS + g - EG + 1)
                            else:
                                act.wait_ge(av_done, START + p * GROUPS)
                        nc.scalar.activation(E[:, (g % EG) * HQ + c, :].rearrange("p (b n) -> p b n", b=NB),
                                             ps, ACT.Exp, bias=negmax[:, i % NM:i % NM + 1], scale=1.0,
                                             accum_out=sums[:, g % EG, c:c + 1]).then_inc(exp_done, 1)
                    elif kind == "z":
                        act.wait_ge(av_done, START + p * GROUPS + (i + 1) * GROUPS // 2)
                        act.wait_ge(filled["u"], START + (p + 1) * NT)
                        nc.scalar.copy(zT[:, i, :].rearrange("p (b n) -> p b n", b=NB), O[:]).then_inc(z_act, 1)
                    elif kind == "u":
                        nc.scalar.activation(ps[:, 0, 0:D], ps[:, 0, 0:D], ACT.Square,
                                             accum_out=ssu[:, i:i + 1]).then_inc(u_act, 1)
                        act.wait_ge(w_dve, p * NT + i + 1)
                        nc.scalar.activation(ps[:, 1, 0:D], ps[:, 1, 0:D], ACT.Square,
                                             accum_out=ssw[:, i:i + 1]).then_inc(w_sq, 1)
                    elif kind == "gelu":
                        act.wait_ge(norm_step, (p + 1) * 5)
                        for t in range(NT):
                            nc.scalar.activation(wb[:, t, 0:D], wb[:, t, 0:D], ACT.Gelu,
                                                 scale=gsc[:, t:t + 1]).then_inc(gelu_done, 1)
                    elif kind == "xt":
                        act.wait_ge(filled["qk"], START + (p + 1) * PER["qk"])
                        act.wait_ge(filled["v"], START + (p + 1) * PER["v"])
                        nc.scalar.copy(XT[:, i, :].rearrange("p (b n) -> p b n", b=NB), ps).then_inc(xt_act, 1)
                    elif kind == "xt2":
                        act.wait_ge(filled["xt"], START + (p + 2) * DC)
                        nc.scalar.copy(XT2[:, i, :].rearrange("p (b n) -> p b n", b=NB), ps).then_inc(xt2_act, 1)
                    elif kind == "qk":
                        if not isinstance(p, int) or i >= 2:
                            act.wait_ge(split_step, (p + 1) * 32 + 4 * (i - 1))
                        nc.scalar.activation(qstage[:, i % 2, :], ps[:, 0, :], ACT.Copy,
                                             scale=SCORE_SCALE if (i // 2) % 2 else 1.0).then_inc(qk_act, 1)
                    elif kind == "v":
                        act.wait_ge(v_swapped, p + 1)
                        nc.scalar.copy(vnext[:, 2 * i:2 * i + 2, :],
                                       ps[:, 0, :].rearrange("p (a n) -> p a n", a=2)).then_inc(v_act, 1)
                    elif kind == "gram":
                        act.wait_ge(filled["G"], START + p)
                        nc.scalar.copy(S[:, i, :], ps[:, 0, 0:D + 1]).then_inc(gram_act, 1)
                    elif kind == "T":
                        act.wait_ge(filled["H"], START + p)
                        nc.scalar.copy(T[:], ps[:, 0, :].rearrange("p (a n) -> p a n", a=2)).then_inc(T_act, 1)
                        nc.scalar.copy(rrow[:], ps[0:1, 1, :]).then_inc(T_act, 1)
                    elif kind == "G":
                        nc.scalar.copy(G[:], ps[:, 0, :].rearrange("p (a n) -> p a n", a=2)).then_inc(G_act, 1)
                    elif kind == "H":
                        act.wait_ge(filled["y"], START + p * PER["y"])
                        nc.scalar.copy(H[:], ps[:, 0, :].rearrange("p (a n) -> p a n", a=2)).then_inc(H_act, 1)

            sections(act, part)

        @block.vector
        def _(dve):
            dve.wait_ge(const_ready, 6)
            nc.vector.tensor_reduce(mask[:], ident[:].rearrange("p (k j) -> p j k", j=AH),
                                    axis=AX.X, op=ALU.add).then_inc(const_dve, 1)
            nc.vector.memset(zT[:], 0.0).then_inc(const_dve, 1)
            nc.vector.memset(wb[:, :, D:D + 1], 1.0).then_inc(const_dve, 1)
            dve.wait_ge(w_loaded, 11 * 16)
            nc.vector.memset(nbrow[:, 0:D], 0.0).then_inc(const_dve, 1)
            for ec in range(DC):
                nc.vector.tensor_copy(wo_perm[:, ec, :].rearrange("p (d h) -> p d h", h=AH),
                                      wo_rows[:, ec, :].rearrange("p (h d) -> p d h", h=AH)
                                      ).then_inc(const_dve, 1)
            nc.vector.tensor_scalar(nbrow[:, D:2 * D], brow[:, D:2 * D], float(N), None,
                                    ALU.mult).then_inc(const_dve, 1)
            nc.vector.tensor_copy(bqb[:], bqc[:].unsqueeze(2).to_broadcast([P, DC, P])).then_inc(const_dve, 1)

            def part(steps, p, linear):
                slot = slots_of(steps)
                for step in steps:
                    kind, i = step[0], index(step)
                    if kind in ("tile", "u", "VK", "H", "y"):
                        dve.wait_ge(filled[kind], START + before(p, kind) + i + 1)
                        ps = ring[:, slot[step][0], :, :]
                    if kind == "tile":
                        nc.vector.tensor_reduce(negmax[:, i % NM:i % NM + 1], ps, axis=AX.XY, op=ALU.max,
                                                negate=True).then_inc(max_ready, 1)
                    elif kind == "v_swap":
                        dve.wait_ge(v_act, START + (p + 1) * PER["v"])
                        dve.wait_ge(vsc_ready, START + p * GROUPS)
                        nc.vector.tensor_copy(vcur[:], vnext[:]).then_inc(v_swapped, 1)
                    elif kind == "recip":
                        dve.wait_ge(exp_done, START + p * TILES + HQ * (i + 1))
                        nc.vector.reciprocal(rsum[:, i % EG, :], sums[:, i % EG, :]).then_inc(rsum_ready, 1)
                    elif kind == "u":
                        dve.wait_ge(filled["xt2"], START + p * DC if linear else LINEAR * DC)
                        nc.vector.tensor_copy(wb[:, i, 0:D], ps[:, 1, 0:D]).then_inc(w_dve, 1)
                    elif kind == "x1":
                        k = NT // 2
                        dve.wait_ge(xr_loaded, (p + 1) * 16)
                        dve.wait_ge(gelu_done, p * NT + (i + 1) * k)
                        nc.vector.scalar_tensor_tensor(
                            out=xr[:, i * k:(i + 1) * k, :], in0=wb[:, i * k:(i + 1) * k, 0:D], scalar=0.5,
                            in1=xr[:, i * k:(i + 1) * k, :], op0=ALU.mult, op1=ALU.add).then_inc(x1_done, 1)
                    elif kind == "ln_stats":
                        dve.wait_ge(xp_loaded, (p + 2) * 16)
                        nc.vector.bn_stats(stats[:, i, :], xp[:, i, :]).then_inc(ln_stats, 1)
                    elif kind == "ln_aggr":
                        dve.wait_ge(ln_stats, (p + 2) * NT)
                        nc.vector.memset(sink[:], 0.0)
                        for t in range(NT):
                            nc.vector.bn_aggr(mv[:, t, :], stats[:, t, :]).then_inc(ln_aggr, 1)
                    elif kind == "ln_rstd":
                        dve.wait_ge(ln_aggr, (p + 2) * NT)
                        nc.vector.tensor_scalar(rstd[:], mv[:, :, 1], LN_EPS, None, ALU.add).then_inc(var_ready, 1)
                    elif kind == "xn":
                        dve.wait_ge(rstd_ready, p + 2)
                        nc.vector.tensor_scalar(xp[:, i, :], xp[:, i, :], mv[:, i, 0:1], rstd[:, i:i + 1],
                                                ALU.subtract, ALU.mult).then_inc(xn_ready, 1)
                    elif kind == "ln2_stats":
                        dve.wait_ge(x1_done, p * 2 + i // 4 + 1)
                        nc.vector.bn_stats(stats2[:, i, :], xr[:, i, :]).then_inc(ln2_stats, 1)
                    elif kind == "ln2_aggr":
                        dve.wait_ge(ln2_stats, (p + 1) * NT)
                        nc.vector.memset(sink[:], 0.0)
                        for t in range(NT):
                            nc.vector.bn_aggr(mv2[:, t, :], stats2[:, t, :]).then_inc(ln2_aggr, 1)
                    elif kind == "ln2_rstd":
                        dve.wait_ge(ln2_aggr, (p + 1) * NT)
                        nc.vector.tensor_scalar(rstd2[:], mv2[:, :, 1], LN_EPS, None, ALU.add).then_inc(var2_ready, 1)
                    elif kind == "u_floor":
                        dve.wait_ge(u_act, (p + 1) * NT)
                        nc.vector.tensor_scalar(ssu[:], ssu[:], NORM_EPS2, None, ALU.max).then_inc(u_floored, 1)
                    elif kind == "w_floor":
                        dve.wait_ge(norm_step, p * 5 + 3)
                        nc.vector.tensor_scalar(ssw[:], ssw[:], NORM_EPS2, None, ALU.max).then_inc(w_floored, 1)
                    elif kind == "xn2":
                        dve.wait_ge(rstd2_ready, p + 1)
                        nc.vector.tensor_scalar(wb[:, i, 0:D], xr[:, i, :], mv2[:, i, 0:1], rstd2[:, i:i + 1],
                                                ALU.subtract, ALU.mult).then_inc(xn2_ready, 1)
                    elif kind == "VK":
                        for jc in range(DC):
                            nc.vector.tensor_tensor(
                                VK[:, jc, 0:D].rearrange("p (k j) -> p k j", j=AH),
                                ps[:, 0, jc * D:(jc + 1) * D].rearrange("p (k j) -> p k j", j=AH),
                                mask[:].unsqueeze(1).to_broadcast([P, D // AH, AH]),
                                ALU.mult).then_inc(VK_dve, 1)
                    elif kind == "H":
                        dve.wait_ge(xbias_done, START + p * 4)
                        nc.vector.tensor_tensor(biasw[:], ps[:, 1, 0:D], bob[:], ALU.add).then_inc(bias_dve, 1)
                    elif kind == "y":
                        dve.wait_ge(xbias_done, START + p * 4 + i + 1)
                        nc.vector.tensor_tensor(
                            xr[:, 2 * i:2 * i + 2, :], ps[:, 0, :].rearrange("p (a n) -> p a n", a=2),
                            xr[:, 2 * i:2 * i + 2, :], ALU.add).then_inc(y_dve, 1)

            sections(dve, part)

        @block.tensor
        def _(pe):
            mm = nc.tensor.matmul
            pe.wait_ge(const_ready, 6)
            pe.wait_ge(w_loaded, 11 * 16)
            for lc in range(DC):
                for mc in range(DC):
                    last = nc.tensor.transpose(ring[:, 0, 0, mc * D + lc * P:mc * D + (lc + 1) * P],
                                               wow[:, lc, mc * P:(mc + 1) * P], ident[:])
            last.then_inc(setup_pe, 1)
            for ic in range(2 * DC):
                for dc in range(DC):
                    last = nc.tensor.transpose(ring[:, 1, dc, ic * P:(ic + 1) * P],
                                               kv_rows[:, ic, dc * P:(dc + 1) * P], ident[:])
            last.then_inc(setup_pe, 1)
            pe.wait_ge(const_dve, 8)
            for ec in range(DC):
                for jc in range(DC):
                    last = nc.tensor.transpose(ring[:, 2, 0, jc * D + ec * P:jc * D + (ec + 1) * P],
                                               wo_perm[:, ec, jc * P:(jc + 1) * P], ident[:])
            last.then_inc(setup_pe, 1)
            pe.wait_ge(setup_act, 1)
            for lc in range(DC):
                for mc in range(DC):
                    last = mm(ring[:, 0, 0, lc * D:(lc + 1) * D], wo_T[:, mc, lc * P:(lc + 1) * P],
                              wff_sb[:, mc, :], start=(mc == 0), stop=(mc == DC - 1))
            last.then_inc(setup_pe, 1)
            pe.wait_ge(setup_act, 4)
            

            def part(steps, p, linear):
                slot = slots_of(steps)
                if not (isinstance(p, int) and p < 0):
                    pe.wait_ge(exp_done, START + p * TILES)
                    pe.wait_ge(v_act, START + (p + 1) * PER["v"])
                for step in steps:
                    kind, i = step[0], index(step)
                    if kind in PSUM_STEPS:
                        where, had = slot[step]
                        ps = ring[:, where, :, :]
                        if had is not None:
                            done = before(p, had[0]) + index(had) + 1
                            for s in FREED[had[0]]:
                                pe.wait_ge(s, START + done * (2 if s in (T_act, VK_dve) else 1))
                    if kind == "tile":
                        q, j, c = i // QT, (i % QT) // HQ, i % HQ
                        if i % QT == 0:
                            pe.wait_ge(stacked[q % 2], p * 2 * STACK + (q // 2 + 1) * STACK)
                        kq = stack[q % 2]
                        for n in range(NB):
                            last = mm(ps[:, n, :], kq[:, 0, c, j * P:(j + 1) * P],
                                      kq[:, 1, c, n * BANK:(n + 1) * BANK], start=True, stop=True)
                        last.then_inc(filled["tile"], 1)
                    elif kind == "av":
                        g, n = i, step[2]
                        q, j = g // QG, g % QG
                        half, a = q // 2, q % 2
                        if n == 0:
                            pe.wait_ge(vsc_ready, START + p * GROUPS + g + 1)
                            if a == 0 and j == 0:
                                pe.wait_ge(z_act, START + p * HALVES + half)
                        for c in range(HQ):
                            last = mm(O[32 * c:32 * c + 32, n, :], vsc[a][:, g % EG, c, :],
                                      E[:, (g % EG) * HQ + c, n * BANK:(n + 1) * BANK],
                                      start=(a == 0 and j == 0), stop=(a == 1 and j == QG - 1))
                        if n == NB - 1:
                            last.then_inc(av_done, 1)
                    elif kind == "u":
                        pe.wait_ge(z_act, START + p * HALVES)
                        for n in range(2):
                            for h in range(HALVES):
                                last = mm(ps[:, n, 0:D], zT[:, h, i * P:(i + 1) * P],
                                          wow[:, h, n * D:(n + 1) * D],
                                          start=(h == 0), stop=(h == HALVES - 1))
                        last.then_inc(filled["u"], 1)
                    elif kind in ("xt", "xt2"):
                        src = xp if kind == "xt" else wb
                        if kind == "xt":
                            pe.wait_ge(xn_ready, (p + 2) * NT)
                        else:
                            pe.wait_ge(xn2_ready, (p + 1) * NT)
                        for t in range(NT):
                            col = (t % 4) * P
                            last = nc.tensor.transpose(ps[:, t // 4, col:col + P],
                                                       src[:, t, i * P:(i + 1) * P], ident[:])
                        last.then_inc(filled[kind], 1)
                    elif kind == "qk":
                        half, m, n = i // 4, (i // 2) % 2, i % 2
                        col = (D if m == 0 else 0) + half * P
                        pe.wait_ge(xt_act, START + (p + 2) * DC)
                        for dc in range(DC):
                            last = mm(ps[:, 0, :], wqkv[:, dc, col:col + P],
                                      XT[:, dc, n * BANK:(n + 1) * BANK], start=(dc == 0), stop=(dc == DC - 1))
                        last.then_inc(filled["qk"], 1)
                    elif kind == "v":
                        pe.wait_ge(xt_act, START + (p + 2) * DC)
                        for k in range(2):
                            t = 2 * i + k
                            for dc in range(DC):
                                last = mm(ps[:, 0, k * D:(k + 1) * D], XT[:, dc, t * P:(t + 1) * P],
                                          wqkv[:, dc, 2 * D:3 * D], start=(dc == 0), stop=(dc == DC - 1))
                        last.then_inc(filled["v"], 1)
                    elif kind == "gram":
                        pe.wait_ge(xn2_ready, (p + 1) * NT)
                        for t in range(NT):
                            last = mm(ps[:, 0, 0:D + 1], wb[:, t, i * P:(i + 1) * P], wb[:, t, :],
                                      start=(t == 0), stop=(t == NT - 1))
                        last.then_inc(filled["gram"], 1)
                    elif kind == "T":
                        pe.wait_ge(gram_act, START + (p + 1) * DC)
                        for mc in range(DC):
                            for kc in range(DC):
                                mm(ps[:, 0, mc * D:(mc + 1) * D], S[:, kc, mc * P:(mc + 1) * P],
                                   wkv[:, kc, 0:D], start=(kc == 0), stop=(kc == DC - 1))
                        for kc in range(DC):
                            mm(ps[0:1, 1, :], S[:, kc, D:D + 1], wkv[:, kc, :],
                               start=(kc == 0), stop=False)
                        mm(ps[0:1, 1, :], ident[0:1, 0:1], nbrow[:],
                           start=False, stop=True).then_inc(filled["T"], 1)
                    elif kind == "VK":
                        pe.wait_ge(T_act, START + (p + 1) * 2)
                        for jc in range(DC):
                            o = ps[:, 0, jc * D:(jc + 1) * D]
                            for dc in range(DC):
                                mm(o, wkv[:, dc, D + jc * P:D + (jc + 1) * P], T[:, dc, :],
                                   start=(dc == 0), stop=False)
                            mm(o, rrow[0:1, D + jc * P:D + (jc + 1) * P], brow[0:1, 0:D],
                               start=False, stop=False)
                            last = mm(o, brow[0:1, D + jc * P:D + (jc + 1) * P], rrow[0:1, 0:D],
                                      start=False, stop=True)
                        last.then_inc(filled["VK"], 1)
                    elif kind == "G":
                        pe.wait_ge(VK_dve, START + (p + 1) * 2)
                        for ic in range(DC):
                            for jc in range(DC):
                                last = mm(ps[:, 0, ic * D:(ic + 1) * D], VK[:, jc, ic * P:(ic + 1) * P],
                                          wop[:, jc, :], start=(jc == 0), stop=(jc == DC - 1))
                        last.then_inc(filled["G"], 1)
                    elif kind == "H":
                        pe.wait_ge(G_act, START + p + 1)
                        for dc in range(DC):
                            for ic in range(DC):
                                mm(ps[:, 0, dc * D:(dc + 1) * D], wqn[:, ic, dc * P:(dc + 1) * P],
                                   G[:, ic, :], start=(ic == 0), stop=(ic == DC - 1))
                        for ic in range(DC):
                            last = mm(ps[:, 1, 0:D], bqb[:, ic, :], G[:, ic, :],
                                      start=(ic == 0), stop=(ic == DC - 1))
                        last.then_inc(filled["H"], 1)
                    elif kind == "y":
                        pe.wait_ge(H_act, START + p + 1)
                        pe.wait_ge(xt2_act, START + (p + 1) * DC)
                        for k in range(2):
                            t = 2 * i + k
                            for dc in range(DC):
                                last = mm(ps[:, 0, k * D:(k + 1) * D], XT2[:, dc, t * P:(t + 1) * P],
                                          H[:, dc, :], start=(dc == 0), stop=(dc == DC - 1))
                        last.then_inc(filled["y"], 1)

            sections(pe, part)


_INS = ['L0_attn_x', 'L0_attn_w_qkv', 'L0_attn_b_qkv', 'L0_attn_w_o', 'L0_attn_b_o', 'L0_ffn_Wq',
        'L0_ffn_Wk', 'L0_ffn_Wv', 'L0_ffn_Wo', 'L0_ffn_Wff']
_OUTS = [((8, 1024, 256), 'float32')]


def kernel(**inputs):
    import numpy as _np
    import concourse.bacc as _bacc
    from concourse import mybir as _mybir
    from concourse.bass_utils import run_bass_kernel_spmd as _run

    nc = _bacc.Bacc("TRN2", target_bir_lowering=False, num_devices=1)
    arrays, args = {}, []
    for name in _INS:
        a = _np.ascontiguousarray(inputs[name])
        arrays[f"in_{name}"] = a
        args.append(nc.dram_tensor(f"in_{name}", a.shape, _mybir.dt.from_np(a.dtype), kind="ExternalInput").ap())
    for i, (shape, dtype) in enumerate(_OUTS):
        dt = _mybir.dt.from_np(_np.dtype(dtype))
        args.append(nc.dram_tensor(f"out_{i}", shape, dt, kind="ExternalOutput").ap())
    build_macaron(nc, *args)
    r = _run(nc, [arrays], core_ids=[0])
    return r.results[0]["out_0"]
```

```python
import concourse.bass as bass
from concourse import mybir
from contextlib import ExitStack


def build_macaron(nc, x_in, w_qkv, b_qkv, w_o, b_o, Wq, Wk, Wv, Wo, Wff, out):
    f32, bf16 = mybir.dt.float32, mybir.dt.bfloat16
    ALU, ACT, AX = mybir.AluOpType, mybir.ActivationFunctionType, mybir.AxisListType

    B, N, D = x_in.shape
    P = 128
    DC = D // P
    NT = N // P
    BANK = 512
    NB = N // BANK
    FH, FD = 16, D // 16
    AH = 8
    QUARTERS = 4
    HQ = FH // QUARTERS
    TILES = FH * NT
    GROUPS = TILES // HQ
    QT = TILES // QUARTERS
    QG = GROUPS // QUARTERS
    HALVES = 2
    EG = 4
    NM = EG * HQ
    SLOTS = 3
    PHASES = 2 * B
    LINEAR = B + 1
    LN_EPS, NORM_EPS2 = 1e-5, 1e-24
    SCORE_SCALE = float(D) ** -0.5
    TERMS = [(0, 0), (0, 1), (1, 0), (1, 1), (0, 2), (2, 0), (1, 2), (2, 1)]
    STACK = 16 * len(TERMS) * HQ
    assert len(TERMS) * FD == P

    xs = nc.dram_tensor("x_slots", (3 * B, N, D), f32, kind="Internal").ap()

    def tokens(rows):
        return rows.rearrange("(t p) d -> p t d", p=P)

    PSUM_STEPS = {"tile", "u", "gram", "xt2", "T", "VK", "G", "H", "y", "xt", "qk", "v"}
    PER = {"tile": TILES, "u": NT, "gram": DC, "xt2": DC, "T": 1, "VK": 1, "G": 1, "H": 1, "y": 4,
           "xt": DC, "qk": 8, "v": 4}

    RECIP, AV, AV_NEXT, OUT_OF_O = 5.7, 9.1, 2, 7.3
    POST = {
        "u": (11.1, 15.5, 16.9, 19.6, 21.8, 26.4, 27.4, 30.1),
        "u_norm": (32.2,),
        "w_norm": (34.1,),
        "gelu": (35.9,),
        "x1": (39.2, 40.5),
    }
    LINEAR_POST = {
        "ln2_stats": (40.3, 40.8, 40.9, 41.1, 43.9, 44.2, 45.4, 45.5),
        "ln2_aggr": (46.4,),
        "ln2_rstd": (48.6,),
        "xn2": (50.3, 51.3, 51.6, 54.3, 55.1, 55.7, 57.4, 59.2),
        "gram": (61.9, 67.4),
        "xt2": (71.1, 103.1),
        "T": (71.8,),
        "VK": (76.1,),
        "G": (81.2,),
        "H": (86.8,),
        "xbias": (87.9, 99.9, 108.1, 109.3),
        "y": (107.9, 111.9, 113.5, 116.3),
    }
    PREP = {
        "ln_stats": (11.6, 16.1, 16.5, 16.8, 20.8, 21.9, 22.1, 25.1),
        "ln_aggr": (26.2,),
        "ln_rstd": (26.4,),
        "xn": (33.5, 35.1, 35.5, 35.5, 35.7, 38.1, 38.7, 39.8),
        "xt": (43.2, 55.8),
        "qk": (89.8, 94.2, 98.4, 102.4),
        "v": (108.7, 119.8, 125.7),
    }
    LATE_PREP = {
        "qk": (23.1, 34.3, 35.1, 38.7),
        "v": (7.4,),
    }

    def section_steps(tiles, prep, post, linear):
        placed = []

        def put(place, *step):
            placed.append((place % TILES, len(placed), step))

        for g in range(GROUPS):
            if tiles or (post and g == GROUPS - 1):
                put(HQ * g + RECIP, "recip", g)
            for n in range(NB):
                if tiles or (post and g >= GROUPS - 2):
                    put(HQ * g + AV + AV_NEXT * n, "av", g, n)
        for half in range(HALVES):
            if tiles or (post and half == 1):
                put(TILES // 2 * (half + 1) + OUT_OF_O, "z", half)
        if tiles:
            for t in range(TILES):
                put(t, "tile", t)
        for wanted, table in ((post, POST), (linear and post, LINEAR_POST), (prep, PREP)):
            for kind, places in table.items():
                for i, place in enumerate(places):
                    if wanted:
                        put(place, kind, i)
        if tiles:
            for kind, places in LATE_PREP.items():
                for i, place in enumerate(places):
                    put(place, kind, PER[kind] - len(places) + i)
        return [step for _, _, step in sorted(placed)]

    prologue = section_steps(False, True, False, False)
    linear_body = section_steps(True, True, True, True)
    plain_body = section_steps(True, True, True, False)
    epilogue = section_steps(False, False, True, False)

    ctx = ExitStack()
    with ctx:
        def sb(name, shape, dt=f32):
            return ctx.enter_context(nc.sbuf_tensor(name, shape, dt))

        def sem(name):
            return ctx.enter_context(nc.semaphore(name))

        wqkv = sb("ffn_wqkv", [P, DC, 3 * D])
        wow = sb("ffn_wo_wowff", [P, DC, 2 * D])
        wkv = sb("attn_wkv", [P, DC, 2 * D])
        wqn = sb("attn_wq_rows", [P, DC, D])
        wop = sb("attn_wo_cols", [P, DC, D])
        brow = sb("attn_bkv_row", [1, 2 * D])
        nbrow = sb("attn_nbv_row", [1, 2 * D])
        bqc = sb("attn_bq_col", [P, DC])
        bqb = sb("attn_bq_wide", [P, DC, P])
        bob = sb("attn_bo_wide", [P, D])
        ident = sb("identity", [P, P])
        mask = sb("head_mask", [P, AH])
        half_neg = sb("minus_half", [P, NT])
        zero = sb("zero", [P, 1])
        E = sb("exp_ring", [P, EG * HQ, N])
        stack = [sb(f"kq_stack{i}", [P, 2, HQ, N], bf16) for i in range(2)]
        parts = sb("kq_parts", [P, 6, N], bf16)
        qstage = sb("kq_stage", [P, 2, BANK])
        resid = sb("kq_rest", [P, BANK])
        vcur = sb("v_now", [P, NT, D])
        vsc = [sb(f"v_scaled{a}", [P, EG, HQ, 2 * FD]) for a in range(2)]
        negmax = sb("neg_max", [P, NM])
        sums = sb("exp_sums", [P, EG, HQ])
        rsum = sb("exp_rsums", [P, EG, HQ])
        zT = sb("o_T", [P, HALVES, N])
        xp = sb("x_prep", [P, NT, D])
        xr = sb("x_post", [P, NT, D])
        XT = sb("xn_T", [P, DC, N])
        XT2 = xp[:].rearrange("p (c t) d -> p c (t d)", c=DC)
        wb = sb("w_xn2", [P, NT, D + 1])
        stats = sb("bn_stats", [P, NT, 6])
        mv = sb("bn_mv", [P, NT, 2])
        rstd = sb("rstd", [P, NT])
        stats2 = sb("bn_stats2", [P, NT, 6])
        mv2 = sb("bn_mv2", [P, NT, 2])
        rstd2 = sb("rstd2", [P, NT])
        ssu = sb("sumsq_u", [P, NT])
        ssw = sb("sumsq_w", [P, NT])
        unorm = sb("u_rnorm", [P, NT])
        sink = sb("wait_sink", [P, 1])
        gsc = sb("gelu_scale", [P, NT])
        S = sb("gram_then_vk", [P, DC, D + 1])
        VK = S
        T = sb("t_then_g", [P, DC, D])
        G = T
        H = sb("h", [P, DC, D])
        rrow = sb("r_row", [1, 2 * D])
        biasw = sb("bias_wide", [P, D])

        ring = ctx.enter_context(nc.psum_tensor("ring", [P, SLOTS, NB, BANK], f32))
        O = ctx.enter_context(nc.psum_tensor("o_acc", [P, NB, BANK], f32))

        tmp = E[:, 0, :].rearrange("p (a n) -> p a n", a=4)
        wo_T, wff_sb = tmp[:, 0:2, :], tmp[:, 2:4, :]
        kv_rows = E[:, 1, :].rearrange("p (a n) -> p a n", a=4)
        wo_rows = E[:, 2, 0:2 * D].rearrange("p (a n) -> p a n", a=2)
        wo_perm = E[:, 2, 2 * D:4 * D].rearrange("p (a n) -> p a n", a=2)

        w_loaded = sem("w_loaded")
        x_copied = sem("x_copied")
        xp_loaded = sem("xp_loaded")
        xr_loaded = sem("xr_loaded")
        x_stored = sem("x_stored")
        out_stored = sem("out_stored")
        stacked = [sem(f"stacked{i}") for i in range(2)]
        const_ready = sem("const_ready")
        const_dve = sem("const_dve")
        setup_pe = sem("setup_pe")
        setup_act = sem("setup_act")
        filled = {k: sem(f"filled_{k}") for k in sorted(PSUM_STEPS)}
        max_ready = sem("max_ready")
        exp_done = sem("exp_done")
        rsum_ready = sem("rsum_ready")
        vsc_ready = sem("vsc_ready")
        av_done = sem("av_done")
        z_dve = sem("z_dve")
        u_act = sem("u_act")
        w_sq = sem("w_sq")
        w_dve = sem("w_dve")
        u_floored = sem("u_floored")
        w_floored = sem("w_floored")
        norm_step = sem("norm_step")
        var_ready = sem("var_ready")
        var2_ready = sem("var2_ready")
        gelu_done = sem("gelu_done")
        x1_done = sem("x1_done")
        ln_stats = sem("ln_stats")
        ln_aggr = sem("ln_aggr")
        rstd_ready = sem("rstd_ready")
        xn_ready = sem("xn_ready")
        xt_act = sem("xt_act")
        qk_act = sem("qk_act")
        split_step = sem("split_step")
        v_act = sem("v_act")
        ln2_stats = sem("ln2_stats")
        ln2_aggr = sem("ln2_aggr")
        rstd2_ready = sem("rstd2_ready")
        xn2_ready = sem("xn2_ready")
        xt2_act = sem("xt2_act")
        gram_act = sem("gram_act")
        T_act = sem("T_act")
        VK_dve = sem("VK_dve")
        G_act = sem("G_act")
        H_act = sem("H_act")
        bias_dve = sem("bias_dve")
        xbias_done = sem("xbias_done")
        y_dve = sem("y_dve")

        FREED = {"tile": [max_ready], "u": [w_sq], "gram": [gram_act], "xt2": [xt2_act],
                 "T": [T_act], "VK": [VK_dve], "G": [G_act], "H": [H_act, bias_dve],
                 "y": [y_dve], "xt": [xt_act], "qk": [qk_act], "v": [v_act]}
        START = 2
        COUNT_FROM_START = [*filled.values(), *dict.fromkeys(s for k in FREED for s in FREED[k]),
                            exp_done, x_stored, out_stored, av_done, z_dve, vsc_ready, xbias_done]
        AHEAD = {"xt": DC, "qk": 4, "v": 3}

        def before(p, kind):
            return p * PER[kind] + AHEAD.get(kind, 0) if not (isinstance(p, int) and p < 0) else 0

        def ranks(steps):
            found, n = {}, {}
            for s in steps:
                if len(s) < 3 or s[2] == 0:
                    n[s[0]] = n.get(s[0], -1) + 1
                found[s] = n[s[0]]
            return found

        def index(step):
            return step[1] if len(step) > 1 else 0

        def av_count(p, g):
            return START + p * GROUPS + g + 3

        LAST_SLOTS = [("last",) + s for s in linear_body if s[0] in PSUM_STEPS][-SLOTS:]
        assert LAST_SLOTS == [("last",) + s for s in plain_body if s[0] in PSUM_STEPS][-SLOTS:]
        assert LAST_SLOTS[0][1] == prologue[-1][0] == "v"
        for steps in (prologue, linear_body, plain_body):
            assert len([s for s in steps if s[0] in PSUM_STEPS]) % SLOTS == 0

        def slot_done(p, rank, step):
            if step[0] == "last":
                kind = step[1]
                return before(p, kind) - PER[kind] + 1 + ranks(linear_body)[step[1:]]
            return before(p, step[0]) + rank[step] + 1

        def slots_of(steps):
            found, n = {}, 0
            had = {} if steps is prologue else dict(enumerate(LAST_SLOTS))
            for s in steps:
                if s[0] in PSUM_STEPS:
                    found[s] = (n % SLOTS, had.get(n % SLOTS))
                    had[n % SLOTS] = s
                    n += 1
            return found

        def sections(engine, part):
            part(prologue, -1, True)
            with engine.Fori(0, LINEAR) as p:
                part(linear_body, p, True)
            with engine.Fori(LINEAR, PHASES) as p:
                part(plain_body, p, False)
            part(epilogue, PHASES, False)

        block = ctx.enter_context(nc.Block())

        @block.sync
        def _(sp):
            for s in COUNT_FROM_START:
                sp.sem_inc(s, START)
            sp.dma_start(xp[:], tokens(x_in[0])).then_inc(xp_loaded, 16)
            for i, w in enumerate((Wq, Wk, Wv)):
                sp.dma_start(wqkv[:, :, i * D:(i + 1) * D],
                             w.rearrange("(c p) n -> p c n", p=P)).then_inc(w_loaded, 16)
            sp.dma_start(wow[:, :, 0:D], Wo.rearrange("(c p) n -> p c n", p=P)).then_inc(w_loaded, 16)
            sp.dma_start(wff_sb, Wff.rearrange("(c p) n -> p c n", p=P)).then_inc(w_loaded, 16)
            sp.dma_start(wqn[:], w_qkv[0:D].rearrange("(c p) n -> p c n", p=P)).then_inc(w_loaded, 16)
            sp.dma_start(kv_rows, w_qkv[D:3 * D].rearrange("(c p) n -> p c n", p=P)).then_inc(w_loaded, 16)
            sp.dma_start(wo_rows, w_o.rearrange("(c p) n -> p c n", p=P)).then_inc(w_loaded, 16)
            sp.dma_start(brow[:], b_qkv[D:3 * D].rearrange("(a n) -> a n", a=1)).then_inc(w_loaded, 16)
            sp.dma_start(bqc[:], b_qkv[0:D].rearrange("(c p) -> p c", p=P), allow_slow_non_contiguous=True).then_inc(w_loaded, 16)
            sp.dma_start(bob[:], b_o.rearrange("(a n) -> a n", a=1).to_broadcast([P, D])).then_inc(w_loaded, 16)
            sp.dma_start(xs[PHASES - 1], x_in[0]).then_inc(x_copied, 16)
            sp.dma_start(xs[0:B], x_in).then_inc(x_copied, 16)

            def stack_quarter(q):
                for t, (kp, qp) in enumerate(TERMS):
                    for c in range(HQ):
                        rows = FD * (2 * c + q % 2)
                        sp.dma_start(stack[q % 2][FD * t:FD * (t + 1), :, c, :],
                                     parts[rows:rows + FD, kp:qp + 4:3 + qp - kp, :]
                                     ).then_inc(stacked[q % 2], 16)

            sp.wait_ge(split_step, 16)
            stack_quarter(0)

            def phase(p, linear):
                if linear:
                    sp.wait_ge(x_stored, START + p * 16)
                    sp.wait_ge(x_copied, 32)
                    sp.dma_start(xr[:], tokens(xs[(p + PHASES - 1) % PHASES])).then_inc(xr_loaded, 16)
                else:
                    sp.wait_ge(x_stored, START + LINEAR * 16)
                    sp.wait_ge(out_stored, START + (p - LINEAR) * 16)
                    sp.dma_start(xr[:], tokens(xs[p - 1])).then_inc(xr_loaded, 16)
                sp.wait_ge(filled["y"], START + (p if linear else LINEAR) * 4)
                sp.wait_ge(filled["xt"], START + (p + 1) * DC)
                sp.dma_start(xp[:], tokens(xs[(p + 1) % PHASES])).then_inc(xp_loaded, 16)
                sp.wait_ge(filled["tile"], START + p * TILES)
                stack_quarter(1)
                sp.wait_ge(split_step, (p + 1) * 32)
                stack_quarter(2)
                sp.wait_ge(filled["tile"], START + p * TILES + 2 * QT)
                stack_quarter(3)
                sp.wait_ge(split_step, (p + 1) * 32 + 16)
                stack_quarter(0)
                if linear:
                    sp.wait_ge(y_dve, START + (p + 1) * 4)
                    sp.dma_start(tokens(xs[(p + PHASES - 1) % PHASES + B]), xr[:]).then_inc(x_stored, 16)
                else:
                    sp.wait_ge(x1_done, (p + 1) * 2)
                    sp.dma_start(tokens(out[p - LINEAR]), xr[:]).then_inc(out_stored, 16)

            sp.wait_ge(x_copied, 32)
            with sp.Fori(0, LINEAR) as p:
                phase(p, True)
            with sp.Fori(LINEAR, PHASES) as p:
                phase(p, False)
            sp.wait_ge(out_stored, START + (B - 1) * 16)
            sp.dma_start(xr[:], tokens(xs[PHASES - 1])).then_inc(xr_loaded, 16)
            sp.wait_ge(x1_done, (PHASES + 1) * 2)
            sp.dma_start(tokens(out[B - 1]), xr[:]).then_inc(out_stored, 16)
            sp.wait_ge(out_stored, START + B * 16)
            sp.wait_ge(stacked[0], (2 * PHASES + 1) * STACK)
            sp.wait_ge(xp_loaded, (PHASES + 1) * 16)

        @block.gpsimd
        def _(pool):
            nc.gpsimd.memset(ident[:], 0.0).then_inc(const_ready, 1)
            pool.wait_ge(const_ready, 1)
            nc.gpsimd.affine_select(out=ident[:], in_=ident[:], compare_op=ALU.not_equal, fill=1.0,
                                    base=0, pattern=[[-1, P]], channel_multiplier=1).then_inc(const_ready, 1)
            nc.gpsimd.memset(half_neg[:], -0.5).then_inc(const_ready, 1)
            nc.gpsimd.memset(zero[:], 0.0).then_inc(const_ready, 1)
            for a in range(2):
                nc.gpsimd.memset(vsc[a][:], 0.0).then_inc(const_ready, 1)
            nc.gpsimd.memset(vcur[:, NT - 1, :], 0.0).then_inc(const_ready, 1)
            pool.wait_ge(const_ready, 7)

            def part(steps, p, linear):
                rank = ranks(steps)
                for step in steps:
                    kind, i, r = step[0], index(step), rank[step]
                    if kind == "ln_rstd":
                        pool.wait_ge(var_ready, p + 2)
                        nc.gpsimd.tensor_tensor(rstd[:], rstd[:], half_neg[:], ALU.pow).then_inc(rstd_ready, 1)
                    elif kind == "ln2_rstd":
                        pool.wait_ge(var2_ready, p + 1)
                        nc.gpsimd.tensor_tensor(rstd2[:], rstd2[:], half_neg[:], ALU.pow).then_inc(rstd2_ready, 1)
                    elif kind == "qk":
                        half, m, n = i // 4, (i // 2) % 2, i % 2
                        piece, rest = qstage[:, r % 2, :], resid[:]
                        zeros = zero[:, 0:1].to_broadcast([P, BANK])

                        def to(k):
                            return parts[:, 3 * m + k, n * BANK:(n + 1) * BANK]

                        at = (before(p, "qk") + r) * 4
                        pool.wait_ge(qk_act, START + before(p, "qk") + r + 1)
                        if i % 4 == 0 and steps is not prologue:
                            for s in stacked:
                                pool.wait_ge(s, (p * 2 + (1 if half else 2)) * STACK)
                        nc.gpsimd.tensor_tensor(to(0), piece, zeros, ALU.add).then_inc(split_step, 1)
                        pool.wait_ge(split_step, at + 1)
                        nc.gpsimd.tensor_tensor(rest, piece, to(0), ALU.subtract).then_inc(split_step, 1)
                        pool.wait_ge(split_step, at + 2)
                        nc.gpsimd.tensor_tensor(to(1), rest, zeros, ALU.add).then_inc(split_step, 1)
                        pool.wait_ge(split_step, at + 3)
                        nc.gpsimd.tensor_tensor(to(2), rest, to(1), ALU.subtract).then_inc(split_step, 1)
                        pool.wait_ge(split_step, at + 4)
                    elif kind == "recip":
                        g = i
                        q, j = g // QG, g % QG
                        half, a = q // 2, q % 2
                        pool.wait_ge(rsum_ready, p * GROUPS + r + 1)
                        if g in (0, 6):
                            pool.wait_ge(v_act, START + before(p, "v") + (1 if g == 6 else 0))
                        heads = vcur[:, j, half * P:(half + 1) * P].rearrange(
                            "p (c a d) -> p c a d", c=HQ, a=2)[:, :, a, :]
                        nc.gpsimd.tensor_tensor(
                            vsc[a][:, g % EG, :, a * FD:(a + 1) * FD], heads,
                            rsum[:, g % EG, :].unsqueeze(2).to_broadcast([P, HQ, FD]),
                            ALU.mult).then_inc(vsc_ready, 1)
                    elif kind == "u_norm":
                        a = unorm[:]
                        pool.wait_ge(u_floored, p + 1)
                        nc.gpsimd.tensor_tensor(a, ssu[:], half_neg[:], ALU.pow).then_inc(norm_step, 1)
                        pool.wait_ge(w_sq, START + (p + 1) * NT)
                        pool.wait_ge(norm_step, p * 5 + 1)
                        nc.gpsimd.tensor_tensor(ssw[:], ssw[:], a, ALU.mult).then_inc(norm_step, 1)
                        pool.wait_ge(norm_step, p * 5 + 2)
                        nc.gpsimd.tensor_tensor(ssw[:], ssw[:], a, ALU.mult).then_inc(norm_step, 1)
                    elif kind == "w_norm":
                        pool.wait_ge(w_floored, p + 1)
                        nc.gpsimd.tensor_tensor(ssw[:], ssw[:], half_neg[:], ALU.pow).then_inc(norm_step, 1)
                        pool.wait_ge(norm_step, p * 5 + 4)
                        nc.gpsimd.tensor_tensor(gsc[:], ssw[:], unorm[:], ALU.mult).then_inc(norm_step, 1)
                    elif kind == "xbias":
                        pool.wait_ge(bias_dve, START + p + 1)
                        pool.wait_ge(x1_done, (p + 1) * 2)
                        nc.gpsimd.tensor_tensor(
                            xr[:, 2 * i:2 * i + 2, :], xr[:, 2 * i:2 * i + 2, :],
                            biasw[:].unsqueeze(1).to_broadcast([P, 2, D]), ALU.add).then_inc(xbias_done, 1)

            sections(pool, part)

        @block.scalar
        def _(act):
            act.wait_ge(setup_pe, 1)
            nc.scalar.copy(wo_T, ring[:, 0, 0, :].rearrange("p (a n) -> p a n", a=2)).then_inc(setup_act, 1)
            act.wait_ge(setup_pe, 2)
            nc.scalar.copy(wkv[:], ring[:, 1, :, :]).then_inc(setup_act, 1)
            act.wait_ge(setup_pe, 3)
            nc.scalar.copy(wop[:], ring[:, 2, 0, :].rearrange("p (a n) -> p a n", a=2)).then_inc(setup_act, 1)
            act.wait_ge(setup_pe, 4)
            nc.scalar.copy(wow[:, :, D:2 * D],
                           ring[:, 0, 0, :].rearrange("p (a n) -> p a n", a=2)).then_inc(setup_act, 1)

            def part(steps, p, linear):
                slot, rank = slots_of(steps), ranks(steps)
                for step in steps:
                    kind, i, r = step[0], index(step), rank[step]
                    if kind in filled and kind not in ("tile", "y", "VK"):
                        act.wait_ge(filled[kind], START + before(p, kind) + r + 1)
                        ps = ring[:, slot[step][0], :, :]
                    if kind == "tile":
                        g, c = i // HQ, i % HQ
                        act.wait_ge(max_ready, START + p * TILES + i + 1)
                        e = E[:, (g % EG) * HQ + c, :]
                        nc.scalar.activation(e, e, ACT.Exp, bias=negmax[:, i % NM:i % NM + 1], scale=-1.0,
                                             accum_out=sums[:, g % EG, c:c + 1]).then_inc(exp_done, 1)
                    elif kind == "u":
                        nc.scalar.activation(ps[:, 0, 0:D], ps[:, 0, 0:D], ACT.Square,
                                             accum_out=ssu[:, i:i + 1]).then_inc(u_act, 1)
                        act.wait_ge(w_dve, p * NT + i + 1)
                        nc.scalar.activation(ps[:, 1, 0:D], ps[:, 1, 0:D], ACT.Square,
                                             accum_out=ssw[:, i:i + 1]).then_inc(w_sq, 1)
                    elif kind == "gelu":
                        act.wait_ge(norm_step, (p + 1) * 5)
                        for t in range(NT):
                            nc.scalar.activation(wb[:, t, 0:D], wb[:, t, 0:D], ACT.Gelu,
                                                 scale=gsc[:, t:t + 1]).then_inc(gelu_done, 1)
                    elif kind == "xt":
                        act.wait_ge(filled["qk"], START + (p + 1) * PER["qk"])
                        act.wait_ge(filled["v"], START + (p + 1) * PER["v"])
                        nc.scalar.copy(XT[:, i, :].rearrange("p (b n) -> p b n", b=NB), ps).then_inc(xt_act, 1)
                    elif kind == "xt2":
                        act.wait_ge(filled["xt"], START + (p + 2) * DC)
                        nc.scalar.copy(XT2[:, i, :].rearrange("p (b n) -> p b n", b=NB), ps).then_inc(xt2_act, 1)
                    elif kind == "qk":
                        if steps is not prologue or r >= 2:
                            act.wait_ge(split_step, (before(p, "qk") + r - 1) * 4)
                        nc.scalar.activation(qstage[:, r % 2, :], ps[:, 0, :], ACT.Copy,
                                             scale=SCORE_SCALE if (i // 2) % 2 else 1.0).then_inc(qk_act, 1)
                    elif kind == "v":
                        if i == 3:
                            act.wait_ge(vsc_ready, START + p * GROUPS + 1)
                        elif steps is not prologue:
                            act.wait_ge(vsc_ready, START + p * GROUPS + 3 * QG + 2 * i + 1 + 2)
                        nc.scalar.copy(vcur[:, 2 * i:2 * i + 2, :],
                                       ps[:, 0, :].rearrange("p (a n) -> p a n", a=2)).then_inc(v_act, 1)
                    elif kind == "gram":
                        act.wait_ge(filled["G"], START + p)
                        nc.scalar.copy(S[:, i, :], ps[:, 0, 0:D + 1]).then_inc(gram_act, 1)
                    elif kind == "T":
                        act.wait_ge(filled["H"], START + p)
                        nc.scalar.copy(T[:], ps[:, 0, :].rearrange("p (a n) -> p a n", a=2)).then_inc(T_act, 1)
                        nc.scalar.copy(rrow[:], ps[0:1, 1, :]).then_inc(T_act, 1)
                    elif kind == "G":
                        nc.scalar.copy(G[:], ps[:, 0, :].rearrange("p (a n) -> p a n", a=2)).then_inc(G_act, 1)
                    elif kind == "H":
                        act.wait_ge(filled["y"], START + p * PER["y"])
                        nc.scalar.copy(H[:], ps[:, 0, :].rearrange("p (a n) -> p a n", a=2)).then_inc(H_act, 1)

            sections(act, part)

        @block.vector
        def _(dve):
            dve.wait_ge(const_ready, 7)
            nc.vector.tensor_reduce(mask[:], ident[:].rearrange("p (k j) -> p j k", j=AH),
                                    axis=AX.X, op=ALU.add).then_inc(const_dve, 1)
            nc.vector.memset(zT[:], 0.0).then_inc(const_dve, 1)
            nc.vector.memset(E[:, 2 * HQ:4 * HQ, :], 0.0).then_inc(const_dve, 1)
            nc.vector.memset(sums[:, EG - 1, :], 1.0).then_inc(const_dve, 1)
            nc.vector.memset(wb[:, :, D:D + 1], 1.0).then_inc(const_dve, 1)
            dve.wait_ge(w_loaded, 11 * 16)
            nc.vector.memset(nbrow[:, 0:D], 0.0).then_inc(const_dve, 1)
            for ec in range(DC):
                nc.vector.tensor_copy(wo_perm[:, ec, :].rearrange("p (d h) -> p d h", h=AH),
                                      wo_rows[:, ec, :].rearrange("p (h d) -> p d h", h=AH)
                                      ).then_inc(const_dve, 1)
            nc.vector.tensor_scalar(nbrow[:, D:2 * D], brow[:, D:2 * D], float(N), None,
                                    ALU.mult).then_inc(const_dve, 1)
            nc.vector.tensor_copy(bqb[:], bqc[:].unsqueeze(2).to_broadcast([P, DC, P])).then_inc(const_dve, 1)

            def part(steps, p, linear):
                slot, rank = slots_of(steps), ranks(steps)
                for step in steps:
                    kind, i, r = step[0], index(step), rank[step]
                    if kind in ("tile", "u", "VK", "H", "y"):
                        dve.wait_ge(filled[kind], START + before(p, kind) + r + 1)
                        ps = ring[:, slot[step][0], :, :]
                    if kind == "tile":
                        g, c = i // HQ, i % HQ
                        if c == 0:
                            had = av_count(p, g - EG)
                            dve.wait_ge(av_done, had)
                        nc.vector.tensor_scalar(
                            E[:, (g % EG) * HQ + c, :].rearrange("p (b n) -> p b n", b=NB), ps, -1.0, None,
                            ALU.mult, ALU.min, accum_out=negmax[:, i % NM:i % NM + 1]).then_inc(max_ready, 1)
                    elif kind == "z":
                        if i == 1:
                            dve.wait_ge(av_done, av_count(p - 1, GROUPS - 1))
                            dve.wait_ge(filled["u"], START + p * NT)
                        else:
                            dve.wait_ge(av_done, av_count(p, GROUPS // 2 - 1))
                            dve.wait_ge(filled["u"], START + (p + 1) * NT)
                        nc.vector.tensor_copy(zT[:, i, :].rearrange("p (b n) -> p b n", b=NB), O[:]).then_inc(z_dve, 1)
                    elif kind == "recip":
                        dve.wait_ge(exp_done, START + p * TILES + HQ * r)
                        nc.vector.reciprocal(rsum[:, i % EG, :], sums[:, i % EG, :]).then_inc(rsum_ready, 1)
                    elif kind == "u":
                        dve.wait_ge(filled["xt2"], START + p * DC if linear else LINEAR * DC)
                        nc.vector.tensor_copy(wb[:, i, 0:D], ps[:, 1, 0:D]).then_inc(w_dve, 1)
                    elif kind == "x1":
                        k = NT // 2
                        dve.wait_ge(xr_loaded, (p + 1) * 16)
                        dve.wait_ge(gelu_done, p * NT + (i + 1) * k)
                        nc.vector.scalar_tensor_tensor(
                            out=xr[:, i * k:(i + 1) * k, :], in0=wb[:, i * k:(i + 1) * k, 0:D], scalar=0.5,
                            in1=xr[:, i * k:(i + 1) * k, :], op0=ALU.mult, op1=ALU.add).then_inc(x1_done, 1)
                    elif kind == "ln_stats":
                        dve.wait_ge(xp_loaded, (p + 2) * 16)
                        nc.vector.bn_stats(stats[:, i, :], xp[:, i, :]).then_inc(ln_stats, 1)
                    elif kind == "ln_aggr":
                        dve.wait_ge(ln_stats, (p + 2) * NT)
                        nc.vector.memset(sink[:], 0.0)
                        for t in range(NT):
                            nc.vector.bn_aggr(mv[:, t, :], stats[:, t, :]).then_inc(ln_aggr, 1)
                    elif kind == "ln_rstd":
                        dve.wait_ge(ln_aggr, (p + 2) * NT)
                        nc.vector.tensor_scalar(rstd[:], mv[:, :, 1], LN_EPS, None, ALU.add).then_inc(var_ready, 1)
                    elif kind == "xn":
                        dve.wait_ge(rstd_ready, p + 2)
                        nc.vector.tensor_scalar(xp[:, i, :], xp[:, i, :], mv[:, i, 0:1], rstd[:, i:i + 1],
                                                ALU.subtract, ALU.mult).then_inc(xn_ready, 1)
                    elif kind == "ln2_stats":
                        dve.wait_ge(x1_done, p * 2 + i // 4 + 1)
                        nc.vector.bn_stats(stats2[:, i, :], xr[:, i, :]).then_inc(ln2_stats, 1)
                    elif kind == "ln2_aggr":
                        dve.wait_ge(ln2_stats, (p + 1) * NT)
                        nc.vector.memset(sink[:], 0.0)
                        for t in range(NT):
                            nc.vector.bn_aggr(mv2[:, t, :], stats2[:, t, :]).then_inc(ln2_aggr, 1)
                    elif kind == "ln2_rstd":
                        dve.wait_ge(ln2_aggr, (p + 1) * NT)
                        nc.vector.tensor_scalar(rstd2[:], mv2[:, :, 1], LN_EPS, None, ALU.add).then_inc(var2_ready, 1)
                    elif kind == "u_norm":
                        dve.wait_ge(u_act, (p + 1) * NT)
                        nc.vector.tensor_scalar(ssu[:], ssu[:], NORM_EPS2, None, ALU.max).then_inc(u_floored, 1)
                    elif kind == "w_norm":
                        dve.wait_ge(norm_step, p * 5 + 3)
                        nc.vector.tensor_scalar(ssw[:], ssw[:], NORM_EPS2, None, ALU.max).then_inc(w_floored, 1)
                    elif kind == "xn2":
                        dve.wait_ge(rstd2_ready, p + 1)
                        nc.vector.tensor_scalar(wb[:, i, 0:D], xr[:, i, :], mv2[:, i, 0:1], rstd2[:, i:i + 1],
                                                ALU.subtract, ALU.mult).then_inc(xn2_ready, 1)
                    elif kind == "VK":
                        for jc in range(DC):
                            nc.vector.tensor_tensor(
                                VK[:, jc, 0:D].rearrange("p (k j) -> p k j", j=AH),
                                ps[:, 0, jc * D:(jc + 1) * D].rearrange("p (k j) -> p k j", j=AH),
                                mask[:].unsqueeze(1).to_broadcast([P, D // AH, AH]),
                                ALU.mult).then_inc(VK_dve, 1)
                    elif kind == "H":
                        dve.wait_ge(xbias_done, START + p * 4)
                        nc.vector.tensor_tensor(biasw[:], ps[:, 1, 0:D], bob[:], ALU.add).then_inc(bias_dve, 1)
                    elif kind == "y":
                        dve.wait_ge(xbias_done, START + p * 4 + i + 1)
                        nc.vector.tensor_tensor(
                            xr[:, 2 * i:2 * i + 2, :], ps[:, 0, :].rearrange("p (a n) -> p a n", a=2),
                            xr[:, 2 * i:2 * i + 2, :], ALU.add).then_inc(y_dve, 1)

            sections(dve, part)

        @block.tensor
        def _(pe):
            mm = nc.tensor.matmul
            pe.wait_ge(const_ready, 7)
            pe.wait_ge(w_loaded, 11 * 16)
            for lc in range(DC):
                for mc in range(DC):
                    last = nc.tensor.transpose(ring[:, 0, 0, mc * D + lc * P:mc * D + (lc + 1) * P],
                                               wow[:, lc, mc * P:(mc + 1) * P], ident[:])
            last.then_inc(setup_pe, 1)
            for ic in range(2 * DC):
                for dc in range(DC):
                    last = nc.tensor.transpose(ring[:, 1, dc, ic * P:(ic + 1) * P],
                                               kv_rows[:, ic, dc * P:(dc + 1) * P], ident[:])
            last.then_inc(setup_pe, 1)
            pe.wait_ge(const_dve, 10)
            for ec in range(DC):
                for jc in range(DC):
                    last = nc.tensor.transpose(ring[:, 2, 0, jc * D + ec * P:jc * D + (ec + 1) * P],
                                               wo_perm[:, ec, jc * P:(jc + 1) * P], ident[:])
            last.then_inc(setup_pe, 1)
            pe.wait_ge(setup_act, 1)
            for lc in range(DC):
                for mc in range(DC):
                    last = mm(ring[:, 0, 0, lc * D:(lc + 1) * D], wo_T[:, mc, lc * P:(lc + 1) * P],
                              wff_sb[:, mc, :], start=(mc == 0), stop=(mc == DC - 1))
            last.then_inc(setup_pe, 1)
            pe.wait_ge(setup_act, 4)
            for c in range(HQ):
                for n in range(NB):
                    mm(O[32 * c:32 * c + 32, n, :], vsc[1][:, 2, c, :], E[:, 2 * HQ + c, n * BANK:(n + 1) * BANK],
                       start=True, stop=False)

            def part(steps, p, linear):
                slot, rank = slots_of(steps), ranks(steps)
                for step in steps:
                    kind, i, r = step[0], index(step), rank[step]
                    if kind in PSUM_STEPS:
                        where, had = slot[step]
                        ps = ring[:, where, :, :]
                        if had is not None:
                            done = slot_done(p, rank, had)
                            for s in FREED[had[1] if had[0] == "last" else had[0]]:
                                pe.wait_ge(s, START + done * (2 if s in (T_act, VK_dve) else 1))
                    if kind == "tile":
                        q, j, c = i // QT, (i % QT) // HQ, i % HQ
                        if i % QT == 0:
                            pe.wait_ge(stacked[q % 2], p * 2 * STACK + (q // 2 + 1) * STACK)
                        kq = stack[q % 2]
                        for n in range(NB):
                            last = mm(ps[:, n, :], kq[:, 0, c, j * P:(j + 1) * P],
                                      kq[:, 1, c, n * BANK:(n + 1) * BANK], start=True, stop=True)
                        last.then_inc(filled["tile"], 1)
                    elif kind == "av":
                        g, n = i, step[2]
                        q, j = g // QG, g % QG
                        half, a = q // 2, q % 2
                        if n == 0:
                            pe.wait_ge(vsc_ready, START + p * GROUPS + r)
                            if a == 0 and j == 0:
                                pe.wait_ge(z_dve, START + p * HALVES + half + 1)
                        for c in range(HQ):
                            last = mm(O[32 * c:32 * c + 32, n, :], vsc[a][:, g % EG, c, :],
                                      E[:, (g % EG) * HQ + c, n * BANK:(n + 1) * BANK],
                                      start=(a == 0 and j == 0), stop=(a == 1 and j == QG - 1))
                        if n == NB - 1:
                            last.then_inc(av_done, 1)
                    elif kind == "u":
                        pe.wait_ge(z_dve, START + p * HALVES + 1)
                        for n in range(2):
                            for h in range(HALVES):
                                last = mm(ps[:, n, 0:D], zT[:, h, i * P:(i + 1) * P],
                                          wow[:, h, n * D:(n + 1) * D],
                                          start=(h == 0), stop=(h == HALVES - 1))
                        last.then_inc(filled["u"], 1)
                    elif kind in ("xt", "xt2"):
                        src = xp if kind == "xt" else wb
                        if kind == "xt":
                            pe.wait_ge(xn_ready, (p + 2) * NT)
                        else:
                            pe.wait_ge(xn2_ready, (p + 1) * NT)
                        for t in range(NT):
                            col = (t % 4) * P
                            last = nc.tensor.transpose(ps[:, t // 4, col:col + P],
                                                       src[:, t, i * P:(i + 1) * P], ident[:])
                        last.then_inc(filled[kind], 1)
                    elif kind == "qk":
                        half, m, n = i // 4, (i // 2) % 2, i % 2
                        col = (D if m == 0 else 0) + half * P
                        pe.wait_ge(xt_act, START + (p + (1 if half else 2)) * DC)
                        for dc in range(DC):
                            last = mm(ps[:, 0, :], wqkv[:, dc, col:col + P],
                                      XT[:, dc, n * BANK:(n + 1) * BANK], start=(dc == 0), stop=(dc == DC - 1))
                        last.then_inc(filled["qk"], 1)
                    elif kind == "v":
                        pe.wait_ge(xt_act, START + (p + (1 if i == 3 else 2)) * DC)
                        for k in range(2):
                            t = 2 * i + k
                            for dc in range(DC):
                                last = mm(ps[:, 0, k * D:(k + 1) * D], XT[:, dc, t * P:(t + 1) * P],
                                          wqkv[:, dc, 2 * D:3 * D], start=(dc == 0), stop=(dc == DC - 1))
                        last.then_inc(filled["v"], 1)
                    elif kind == "gram":
                        pe.wait_ge(xn2_ready, (p + 1) * NT)
                        for t in range(NT):
                            last = mm(ps[:, 0, 0:D + 1], wb[:, t, i * P:(i + 1) * P], wb[:, t, :],
                                      start=(t == 0), stop=(t == NT - 1))
                        last.then_inc(filled["gram"], 1)
                    elif kind == "T":
                        pe.wait_ge(gram_act, START + (p + 1) * DC)
                        for mc in range(DC):
                            for kc in range(DC):
                                mm(ps[:, 0, mc * D:(mc + 1) * D], S[:, kc, mc * P:(mc + 1) * P],
                                   wkv[:, kc, 0:D], start=(kc == 0), stop=(kc == DC - 1))
                        for kc in range(DC):
                            mm(ps[0:1, 1, :], S[:, kc, D:D + 1], wkv[:, kc, :],
                               start=(kc == 0), stop=False)
                        mm(ps[0:1, 1, :], ident[0:1, 0:1], nbrow[:],
                           start=False, stop=True).then_inc(filled["T"], 1)
                    elif kind == "VK":
                        pe.wait_ge(T_act, START + (p + 1) * 2)
                        for jc in range(DC):
                            o = ps[:, 0, jc * D:(jc + 1) * D]
                            for dc in range(DC):
                                mm(o, wkv[:, dc, D + jc * P:D + (jc + 1) * P], T[:, dc, :],
                                   start=(dc == 0), stop=False)
                            mm(o, rrow[0:1, D + jc * P:D + (jc + 1) * P], brow[0:1, 0:D],
                               start=False, stop=False)
                            last = mm(o, brow[0:1, D + jc * P:D + (jc + 1) * P], rrow[0:1, 0:D],
                                      start=False, stop=True)
                        last.then_inc(filled["VK"], 1)
                    elif kind == "G":
                        pe.wait_ge(VK_dve, START + (p + 1) * 2)
                        for ic in range(DC):
                            for jc in range(DC):
                                last = mm(ps[:, 0, ic * D:(ic + 1) * D], VK[:, jc, ic * P:(ic + 1) * P],
                                          wop[:, jc, :], start=(jc == 0), stop=(jc == DC - 1))
                        last.then_inc(filled["G"], 1)
                    elif kind == "H":
                        pe.wait_ge(G_act, START + p + 1)
                        for dc in range(DC):
                            for ic in range(DC):
                                mm(ps[:, 0, dc * D:(dc + 1) * D], wqn[:, ic, dc * P:(dc + 1) * P],
                                   G[:, ic, :], start=(ic == 0), stop=(ic == DC - 1))
                        for ic in range(DC):
                            last = mm(ps[:, 1, 0:D], bqb[:, ic, :], G[:, ic, :],
                                      start=(ic == 0), stop=(ic == DC - 1))
                        last.then_inc(filled["H"], 1)
                    elif kind == "y":
                        pe.wait_ge(H_act, START + p + 1)
                        pe.wait_ge(xt2_act, START + (p + 1) * DC)
                        for k in range(2):
                            t = 2 * i + k
                            for dc in range(DC):
                                last = mm(ps[:, 0, k * D:(k + 1) * D], XT2[:, dc, t * P:(t + 1) * P],
                                          H[:, dc, :], start=(dc == 0), stop=(dc == DC - 1))
                        last.then_inc(filled["y"], 1)

            sections(pe, part)


_INS = ['L0_attn_x', 'L0_attn_w_qkv', 'L0_attn_b_qkv', 'L0_attn_w_o', 'L0_attn_b_o', 'L0_ffn_Wq',
        'L0_ffn_Wk', 'L0_ffn_Wv', 'L0_ffn_Wo', 'L0_ffn_Wff']
_OUTS = [((8, 1024, 256), 'float32')]


def kernel(**inputs):
    import numpy as _np
    import concourse.bacc as _bacc
    from concourse import mybir as _mybir
    from concourse.bass_utils import run_bass_kernel_spmd as _run

    nc = _bacc.Bacc("TRN2", target_bir_lowering=False, num_devices=1)
    arrays, args = {}, []
    for name in _INS:
        a = _np.ascontiguousarray(inputs[name])
        arrays[f"in_{name}"] = a
        args.append(nc.dram_tensor(f"in_{name}", a.shape, _mybir.dt.from_np(a.dtype), kind="ExternalInput").ap())
    for i, (shape, dtype) in enumerate(_OUTS):
        dt = _mybir.dt.from_np(_np.dtype(dtype))
        args.append(nc.dram_tensor(f"out_{i}", shape, dt, kind="ExternalOutput").ap())
    build_macaron(nc, *args)
    r = _run(nc, [arrays], core_ids=[0])
    return r.results[0]["out_0"]
```

```python
import concourse.bass as bass
from concourse import mybir
from contextlib import ExitStack


def build_macaron(nc, x_in, w_qkv, b_qkv, w_o, b_o, Wq, Wk, Wv, Wo, Wff, out):
    f32, bf16 = mybir.dt.float32, mybir.dt.bfloat16
    ALU, ACT, AX = mybir.AluOpType, mybir.ActivationFunctionType, mybir.AxisListType

    B, N, D = x_in.shape
    P = 128
    DC = D // P
    NT = N // P
    BANK = 512
    NB = N // BANK
    FH, FD = 16, D // 16
    AH = 8
    QUARTERS = 4
    HQ = FH // QUARTERS
    TILES = FH * NT
    GROUPS = TILES // HQ
    QT = TILES // QUARTERS
    QG = GROUPS // QUARTERS
    HALVES = 2
    EG = 4
    NM = EG * HQ
    SLOTS = 3
    PHASES = 2 * B
    LINEAR = B + 1
    LN_EPS, NORM_EPS2 = 1e-5, 1e-24
    SCORE_SCALE = float(D) ** -0.5
    TERMS = [(0, 0), (0, 1), (1, 0), (1, 1), (0, 2), (2, 0), (1, 2), (2, 1)]
    SPLIT_STEPS = 4
    STACK = 16 * len(TERMS) * HQ
    assert len(TERMS) * FD == P

    xs = nc.dram_tensor("x_slots", (PHASES, N, D), f32, kind="Internal").ap()

    def tokens(rows):
        return rows.rearrange("(t p) d -> p t d", p=P)

    PSUM_STEPS = {"tile", "u", "gram", "xt2", "T", "VK", "G", "H", "y", "xt", "qk", "v"}
    PER = {"tile": TILES, "u": NT, "gram": DC, "xt2": DC, "T": 1, "VK": 1, "G": 1, "H": 1, "y": 4,
           "xt": DC, "qk": 8, "v": 4}

    AHEAD = {"xt": DC, "qk": 4, "v": 3}

    PLAIN = {
        "recip": 5.1, "av": 9.1, "av_next": 2, "z": 7.7,
        "u": (14.5, 15.6, 16.8, 27.8, 33.6, 47.7, 53.4, 60.8),
        "u_norm": (63.1,),
        "w_norm": (66.9,),
        "gelu": (67.1,),
        "x1": (72.1, 72.2),
        "ln_stats": (9.4, 12.2, 13.8, 14.1, 14.7, 15.6, 16.5, 16.8),
        "ln_aggr": (21.9,),
        "ln_rstd": (28.4,),
        "xn": (33.3, 33.5, 37.1, 37.6, 41.3, 41.7, 53.3, 60.4),
        "xt": (61.7, 63.5),
        "qk": (73.3, 85.4, 93.6, 101.4, 9.2, 21.2, 37.3, 41.7),
        "v": (110.4, 116.1, 125.9, 7.9),
    }
    WITH_LINEAR = {
        "recip": 5.1, "av": 8.1, "av_next": 2, "z": 6.1,
        "u": (8.9, 9.9, 15.6, 16.3, 17.4, 22.8, 26.9, 27.7),
        "u_norm": (28.1,),
        "w_norm": (31.4,),
        "gelu": (32.8,),
        "x1": (36.1, 36.2),
        "ln2_stats": (36.3, 36.7, 36.8, 36.8, 38.2, 38.4, 38.6, 39.1),
        "ln2_aggr": (42.1,),
        "ln2_rstd": (42.5,),
        "xn2": (45.9, 46.5, 47.2, 47.5, 48.5, 48.9, 49.5, 50.9),
        "gram": (52.4, 58.3),
        "xt2": (63.7, 94.9),
        "T": (63.3,),
        "VK": (70.1,),
        "G": (74.3,),
        "H": (87.7,),
        "xbias": (90.9, 92.1, 105.1, 115.9),
        "y": (103.4, 107.2, 115.9, 119.4),
        "ln_stats": (8.7, 13.9, 15.1, 16.2, 16.8, 17.1, 22.6, 26.5),
        "ln_aggr": (27.2,),
        "ln_rstd": (27.9,),
        "xn": (31.3, 33.1, 34.3, 34.7, 34.7, 34.7, 34.9, 35.1),
        "xt": (45.8, 47.3),
        "qk": (77.8, 82.4, 93.7, 97.4, 31.4, 34.2, 38.7, 42.9),
        "v": (111.4, 121.8, 125.1, 6.3),
    }
    PREP = ("ln_stats", "ln_aggr", "ln_rstd", "xn", "xt", "qk", "v")

    def section_steps(places, tiles, prep, post):
        placed = []

        def put(place, *step):
            placed.append((place % TILES, len(placed), step))

        for g in range(GROUPS):
            if tiles or (post and g == GROUPS - 1):
                put(HQ * g + places["recip"], "recip", g)
            for n in range(NB):
                if tiles or (post and g >= GROUPS - 2):
                    put(HQ * g + places["av"] + places["av_next"] * n, "av", g, n)
        for half in range(HALVES):
            if tiles or (post and half == 1):
                put(TILES // 2 * (half + 1) + places["z"], "z", half)
        if tiles:
            for t in range(TILES):
                put(t, "tile", t)
        for kind in places:
            if kind in ("recip", "av", "av_next", "z"):
                continue
            for i, place in enumerate(places[kind]):
                if kind in PREP and prep and (tiles or i < AHEAD.get(kind, PER.get(kind, NT))):
                    put(place, kind, i)
                if kind not in PREP and post:
                    put(place, kind, i)
        return [step for _, _, step in sorted(placed)]

    prologue = section_steps(PLAIN, False, True, False)
    linear_body = section_steps(WITH_LINEAR, True, True, True)
    plain_body = section_steps(PLAIN, True, True, True)
    epilogue = section_steps(PLAIN, False, False, True)

    ctx = ExitStack()
    with ctx:
        def sb(name, shape, dt=f32):
            return ctx.enter_context(nc.sbuf_tensor(name, shape, dt))

        def sem(name):
            return ctx.enter_context(nc.semaphore(name))

        wqkv = sb("ffn_wqkv", [P, DC, 3 * D])
        wow = sb("ffn_wo_wowff", [P, DC, 2 * D])
        wkv = sb("attn_wkv", [P, DC, 2 * D])
        wqn = sb("attn_wq_rows", [P, DC, D])
        wop = sb("attn_wo_cols", [P, DC, D])
        brow = sb("attn_bkv_row", [1, 2 * D])
        nbk = sb("attn_nbk_row", [1, D])
        bkb = sb("attn_bk_wide", [P, D])
        bqc = sb("attn_bq_col", [P, DC])
        bqb = sb("attn_bq_wide", [P, DC, P])
        bob = sb("attn_bo_wide", [P, D])
        ident = sb("identity", [P, P])
        mask = sb("head_mask", [P, AH])
        half_neg = sb("minus_half", [P, NT])
        zero = sb("zero", [P, 1])
        E = sb("exp_ring", [P, EG * HQ, N])
        stack = [sb(f"kq_stack{i}", [P, 2, HQ, N], bf16) for i in range(2)]
        parts = sb("kq_parts", [P, 6, N], bf16)
        qstage = sb("kq_stage", [P, 2, BANK])
        resid = sb("kq_rest", [P, 2, BANK])
        vcur = sb("v_now", [P, NT, D])
        vsc = [sb(f"v_scaled{a}", [P, EG, HQ, 2 * FD]) for a in range(2)]
        negmax = sb("neg_max", [P, NM])
        sums = sb("exp_sums", [P, EG, HQ])
        rsum = sb("exp_rsums", [P, EG, HQ])
        zT = sb("o_T", [P, HALVES, N])
        xp = sb("x_prep", [P, NT, D])
        xr = sb("x_post", [P, NT, D])
        XT = sb("xn_T", [P, DC, N])
        XT2 = xp[:].rearrange("p (c t) d -> p c (t d)", c=DC)
        wb = sb("w_xn2", [P, NT, D + 1])
        stats = sb("bn_stats", [P, NT, 6])
        mv = sb("bn_mv", [P, NT, 2])
        rstd = sb("rstd", [P, NT])
        stats2 = sb("bn_stats2", [P, NT, 6])
        mv2 = sb("bn_mv2", [P, NT, 2])
        rstd2 = sb("rstd2", [P, NT])
        ssu = sb("sumsq_u", [P, NT])
        ssw = sb("sumsq_w", [P, NT])
        unorm = sb("u_rnorm", [P, NT])
        sink = sb("wait_sink", [P, 1])
        gsc = sb("gelu_scale", [P, NT])
        S = sb("gram_then_vk", [P, DC, D + 1])
        VK = S
        T = sb("t_then_g", [P, DC, D])
        G = T
        H = sb("h", [P, DC, D])
        rrow = sb("r_row", [1, D])
        biasw = sb("bias_wide", [P, D])

        ring = ctx.enter_context(nc.psum_tensor("ring", [P, SLOTS, NB, BANK], f32))
        O = ctx.enter_context(nc.psum_tensor("o_acc", [P, NB, BANK], f32))

        tmp = E[:, 0, :].rearrange("p (a n) -> p a n", a=4)
        wo_T, wff_sb = tmp[:, 0:2, :], tmp[:, 2:4, :]
        kv_rows = E[:, 1, :].rearrange("p (a n) -> p a n", a=4)
        wo_rows = E[:, 2, 0:2 * D].rearrange("p (a n) -> p a n", a=2)
        wo_perm = E[:, 2, 2 * D:4 * D].rearrange("p (a n) -> p a n", a=2)

        wqkv_loaded = sem("wqkv_loaded")
        w_loaded = sem("w_loaded")
        exp_zeroed = sem("exp_zeroed")
        dve_split = sem("dve_split")
        x_copied = sem("x_copied")
        xp_loaded = sem("xp_loaded")
        xr_loaded = sem("xr_loaded")
        x_stored = sem("x_stored")
        out_stored = sem("out_stored")
        stacked = [sem(f"stacked{i}") for i in range(2)]
        stacked_by_pool = sem("stacked_by_pool")
        const_ready = sem("const_ready")
        const_dve = sem("const_dve")
        setup_pe = sem("setup_pe")
        setup_act = sem("setup_act")
        filled = {k: sem(f"filled_{k}") for k in sorted(PSUM_STEPS)}
        max_ready = sem("max_ready")
        exp_done = sem("exp_done")
        rsum_ready = sem("rsum_ready")
        vsc_ready = sem("vsc_ready")
        av_done = sem("av_done")
        z_dve = sem("z_dve")
        u_act = sem("u_act")
        w_sq = sem("w_sq")
        w_dve = sem("w_dve")
        u_floored = sem("u_floored")
        w_floored = sem("w_floored")
        norm_step = sem("norm_step")
        var_ready = sem("var_ready")
        var2_ready = sem("var2_ready")
        gelu_done = sem("gelu_done")
        x1_done = sem("x1_done")
        ln_stats = sem("ln_stats")
        ln_aggr = sem("ln_aggr")
        rstd_ready = sem("rstd_ready")
        xn_ready = sem("xn_ready")
        xt_act = sem("xt_act")
        qk_act = sem("qk_act")
        split_step = sem("split_step")
        v_dve = sem("v_dve")
        ln2_stats = sem("ln2_stats")
        ln2_aggr = sem("ln2_aggr")
        rstd2_ready = sem("rstd2_ready")
        xn2_ready = sem("xn2_ready")
        xt2_act = sem("xt2_act")
        gram_act = sem("gram_act")
        T_dve = sem("T_dve")
        VK_dve = sem("VK_dve")
        G_act = sem("G_act")
        H_act = sem("H_act")
        bias_dve = sem("bias_dve")
        xbias_done = sem("xbias_done")
        y_dve = sem("y_dve")

        FREED = {"tile": [max_ready], "u": [w_sq], "gram": [gram_act], "xt2": [xt2_act],
                 "T": [T_dve], "VK": [VK_dve], "G": [G_act], "H": [H_act, bias_dve],
                 "y": [y_dve], "xt": [xt_act], "qk": [qk_act], "v": [v_dve]}
        LINEAR_COUNTS = {**{filled[k]: PER[k] for k in ("gram", "xt2", "T", "VK", "G", "H", "y")},
                         gram_act: DC, xt2_act: DC, T_dve: 3, VK_dve: 2, G_act: 1, H_act: 1, bias_dve: 1,
                         y_dve: 4, xbias_done: 4, x_stored: 16, ln2_stats: NT, ln2_aggr: NT,
                         var2_ready: 1, rstd2_ready: 1, xn2_ready: NT}
        START = 2
        COUNT_FROM_START = [*filled.values(), *dict.fromkeys(s for k in FREED for s in FREED[k]),
                            exp_done, x_stored, out_stored, av_done, z_dve, vsc_ready, xbias_done]

        def before(p, kind):
            return p * PER[kind] + AHEAD.get(kind, 0) if not (isinstance(p, int) and p < 0) else 0

        def ranks(steps):
            found, n = {}, {}
            for s in steps:
                if len(s) < 3 or s[2] == 0:
                    n[s[0]] = n.get(s[0], -1) + 1
                found[s] = n[s[0]]
            return found

        def linear_before(p, linear):
            return p if linear or (isinstance(p, int) and p == 0) else LINEAR

        def index(step):
            return step[1] if len(step) > 1 else 0

        def av_count(p, g):
            return START + p * GROUPS + g + 3

        LAST_SLOTS = [("last",) + s for s in linear_body if s[0] in PSUM_STEPS][-SLOTS:]
        assert LAST_SLOTS == [("last",) + s for s in plain_body if s[0] in PSUM_STEPS][-SLOTS:]
        assert LAST_SLOTS[0][1] == prologue[-1][0] == "v"
        for steps in (prologue, linear_body, plain_body):
            assert len([s for s in steps if s[0] in PSUM_STEPS]) % SLOTS == 0

        def slot_done(p, rank, step):
            if step[0] == "last":
                kind = step[1]
                return before(p, kind) - PER[kind] + 1 + ranks(linear_body)[step[1:]]
            return before(p, step[0]) + rank[step] + 1

        def slots_of(steps):
            found, n = {}, 0
            had = {} if steps is prologue else dict(enumerate(LAST_SLOTS))
            for s in steps:
                if s[0] in PSUM_STEPS:
                    found[s] = (n % SLOTS, had.get(n % SLOTS))
                    had[n % SLOTS] = s
                    n += 1
            return found

        def sections(engine, part, setup=None):
            part(prologue, -1, False)
            if setup:
                setup()
            part(plain_body, 0, False)
            with engine.Fori(1, LINEAR) as p:
                part(linear_body, p, True)
            with engine.Fori(LINEAR, PHASES) as p:
                part(plain_body, p, False)
            part(epilogue, PHASES, False)

        def split(engine, ops, piece, rest, m, n, done, at):
            zeros = zero[:, 0:1].to_broadcast([P, BANK])
            hi, mid, lo = (parts[:, 3 * m + k, n * BANK:(n + 1) * BANK] for k in range(3))
            ops.tensor_tensor(hi, piece, zeros, ALU.add).then_inc(done, 1)
            engine.wait_ge(done, at + 1)
            ops.tensor_tensor(rest, piece, hi, ALU.subtract).then_inc(done, 1)
            engine.wait_ge(done, at + 2)
            ops.tensor_tensor(mid, rest, zeros, ALU.add).then_inc(done, 1)
            engine.wait_ge(done, at + 3)
            ops.tensor_tensor(lo, rest, mid, ALU.subtract).then_inc(done, 1)
            engine.wait_ge(done, at + 4)

        def stack_quarter(queue, q, heads=range(HQ), done=stacked):
            for t, (kp, qp) in enumerate(TERMS):
                for c in heads:
                    rows = FD * (2 * c + q % 2)
                    queue.dma_start(stack[q % 2][FD * t:FD * (t + 1), :, c, :],
                                    parts[rows:rows + FD, kp:qp + 4:3 + qp - kp, :]
                                    ).then_inc(done[q % 2], 16)

        block = ctx.enter_context(nc.Block())

        @block.sync
        def _(sp):
            for s in COUNT_FROM_START:
                sp.sem_inc(s, START)
            for s, count in LINEAR_COUNTS.items():
                sp.sem_inc(s, count)
            sp.sem_inc(split_step, 2 * SPLIT_STEPS)
            sp.sem_inc(stacked[0], STACK // HQ)
            sp.dma_start(xp[:], tokens(x_in[0])).then_inc(xp_loaded, 16)
            for i, w in enumerate((Wq, Wk, Wv)):
                sp.dma_start(wqkv[:, :, i * D:(i + 1) * D],
                             w.rearrange("(c p) n -> p c n", p=P)).then_inc(wqkv_loaded, 16)
            sp.dma_start(wow[:, :, 0:D], Wo.rearrange("(c p) n -> p c n", p=P)).then_inc(w_loaded, 16)
            sp.dma_start(wff_sb, Wff.rearrange("(c p) n -> p c n", p=P)).then_inc(w_loaded, 16)
            sp.dma_start(wqn[:], w_qkv[0:D].rearrange("(c p) n -> p c n", p=P)).then_inc(w_loaded, 16)
            sp.dma_start(kv_rows, w_qkv[D:3 * D].rearrange("(c p) n -> p c n", p=P)).then_inc(w_loaded, 16)
            sp.dma_start(wo_rows, w_o.rearrange("(c p) n -> p c n", p=P)).then_inc(w_loaded, 16)
            sp.dma_start(brow[:], b_qkv[D:3 * D].rearrange("(a n) -> a n", a=1)).then_inc(w_loaded, 16)
            sp.dma_start(bqc[:], b_qkv[0:D].rearrange("(c p) -> p c", p=P), allow_slow_non_contiguous=True).then_inc(w_loaded, 16)
            sp.dma_start(bkb[:], b_qkv[D:2 * D].rearrange("(a n) -> a n", a=1).to_broadcast([P, D])).then_inc(w_loaded, 16)
            sp.dma_start(bob[:], b_o.rearrange("(a n) -> a n", a=1).to_broadcast([P, D])).then_inc(w_loaded, 16)
            sp.dma_start(xs[0:B], x_in).then_inc(x_copied, 16)

            sp.wait_ge(split_step, AHEAD["qk"] * SPLIT_STEPS)
            sp.wait_ge(dve_split, 2 * SPLIT_STEPS)
            stack_quarter(sp, 0, range(HQ - 1))

            def phase(p, linear):
                sp.wait_ge(filled["y"], START + linear_before(p, linear) * PER["y"])
                sp.wait_ge(filled["xt"], START + (p + 1) * DC)
                sp.dma_start(xp[:], tokens(xs[(p + 1) % PHASES])).then_inc(xp_loaded, 16)
                sp.wait_ge(filled["tile"], START + p * TILES)
                stack_quarter(sp, 1)
                if linear or isinstance(p, int):
                    sp.wait_ge(x_stored, START + p * 16)
                else:
                    sp.wait_ge(x_stored, START + LINEAR * 16)
                    sp.wait_ge(out_stored, START + (p - LINEAR) * 16)
                sp.dma_start(xr[:], tokens(xs[0 if isinstance(p, int) else p - 1])).then_inc(xr_loaded, 16)
                sp.wait_ge(split_step, (p + 1) * 32)
                stack_quarter(sp, 2)
                sp.wait_ge(filled["tile"], START + p * TILES + 2 * QT)
                stack_quarter(sp, 3)
                if isinstance(p, int):
                    sp.wait_ge(x1_done, 2)
                elif not linear:
                    sp.wait_ge(x1_done, (p + 1) * 2)
                    sp.dma_start(tokens(out[p - LINEAR]), xr[:]).then_inc(out_stored, 16)
                sp.wait_ge(split_step, (p + 1) * 32 + 16)
                stack_quarter(sp, 0)
                if linear:
                    sp.wait_ge(y_dve, START + (p + 1) * 4)
                    sp.dma_start(tokens(xs[p - 1 + B]), xr[:]).then_inc(x_stored, 16)

            sp.wait_ge(x_copied, 16)
            phase(0, False)
            with sp.Fori(1, LINEAR) as p:
                phase(p, True)
            with sp.Fori(LINEAR, PHASES) as p:
                phase(p, False)
            sp.wait_ge(out_stored, START + (B - 1) * 16)
            sp.dma_start(xr[:], tokens(xs[PHASES - 1])).then_inc(xr_loaded, 16)
            sp.wait_ge(x1_done, (PHASES + 1) * 2)
            sp.dma_start(tokens(out[B - 1]), xr[:]).then_inc(out_stored, 16)
            sp.wait_ge(out_stored, START + B * 16)
            sp.wait_ge(stacked[0], (2 * PHASES + 1) * STACK)
            sp.wait_ge(xp_loaded, (PHASES + 1) * 16)

        @block.gpsimd
        def _(pool):
            nc.gpsimd.memset(ident[:], 0.0).then_inc(const_ready, 1)
            pool.wait_ge(const_ready, 1)
            nc.gpsimd.affine_select(out=ident[:], in_=ident[:], compare_op=ALU.not_equal, fill=1.0,
                                    base=0, pattern=[[-1, P]], channel_multiplier=1).then_inc(const_ready, 1)
            nc.gpsimd.memset(half_neg[:], -0.5).then_inc(const_ready, 1)
            nc.gpsimd.memset(zero[:], 0.0).then_inc(const_ready, 1)
            for a in range(2):
                nc.gpsimd.memset(vsc[a][:], 0.0).then_inc(const_ready, 1)
            nc.gpsimd.memset(vcur[:, NT - 1, :], 0.0).then_inc(const_ready, 1)
            nc.gpsimd.memset(E[:, 2 * HQ:4 * HQ, :], 0.0).then_inc(exp_zeroed, 1)
            pool.wait_ge(const_ready, 7)

            def part(steps, p, linear):
                rank = ranks(steps)
                for step in steps:
                    kind, i, r = step[0], index(step), rank[step]
                    if kind == "ln_rstd":
                        pool.wait_ge(var_ready, p + 2)
                        nc.gpsimd.tensor_tensor(rstd[:], rstd[:], half_neg[:], ALU.pow).then_inc(rstd_ready, 1)
                    elif kind == "ln2_rstd":
                        pool.wait_ge(var2_ready, p + 1)
                        nc.gpsimd.tensor_tensor(rstd2[:], rstd2[:], half_neg[:], ALU.pow).then_inc(rstd2_ready, 1)
                    elif kind == "qk":
                        if steps is prologue and i % 2 == 1:
                            continue
                        half, m, n = i // 4, (i // 2) % 2, i % 2
                        at = SPLIT_STEPS * (2 + i // 2 if steps is prologue else before(p, "qk") + r)
                        pool.wait_ge(qk_act, START + before(p, "qk") + r + 1)
                        if i % 4 == 0 and steps is not prologue:
                            for s in stacked:
                                pool.wait_ge(s, (p * 2 + (1 if half else 2)) * STACK)
                        split(pool, nc.gpsimd, qstage[:, r % 2, :], resid[:, 0, :], m, n, split_step, at)
                    elif kind == "recip":
                        g = i
                        q, j = g // QG, g % QG
                        half, a = q // 2, q % 2
                        pool.wait_ge(rsum_ready, p * GROUPS + r + 1)
                        if g in (0, 6):
                            pool.wait_ge(v_dve, START + before(p, "v") + (1 if g == 6 else 0))
                        heads = vcur[:, j, half * P:(half + 1) * P].rearrange(
                            "p (c a d) -> p c a d", c=HQ, a=2)[:, :, a, :]
                        nc.gpsimd.tensor_tensor(
                            vsc[a][:, g % EG, :, a * FD:(a + 1) * FD], heads,
                            rsum[:, g % EG, :].unsqueeze(2).to_broadcast([P, HQ, FD]),
                            ALU.mult).then_inc(vsc_ready, 1)
                    elif kind == "u_norm":
                        a = unorm[:]
                        pool.wait_ge(u_floored, p + 1)
                        nc.gpsimd.tensor_tensor(a, ssu[:], half_neg[:], ALU.pow).then_inc(norm_step, 1)
                        pool.wait_ge(w_sq, START + (p + 1) * NT)
                        pool.wait_ge(norm_step, p * 5 + 1)
                        nc.gpsimd.tensor_tensor(ssw[:], ssw[:], a, ALU.mult).then_inc(norm_step, 1)
                        pool.wait_ge(norm_step, p * 5 + 2)
                        nc.gpsimd.tensor_tensor(ssw[:], ssw[:], a, ALU.mult).then_inc(norm_step, 1)
                    elif kind == "w_norm":
                        pool.wait_ge(w_floored, p + 1)
                        nc.gpsimd.tensor_tensor(ssw[:], ssw[:], half_neg[:], ALU.pow).then_inc(norm_step, 1)
                        pool.wait_ge(norm_step, p * 5 + 4)
                        nc.gpsimd.tensor_tensor(gsc[:], ssw[:], unorm[:], ALU.mult).then_inc(norm_step, 1)
                    elif kind == "xbias":
                        pool.wait_ge(bias_dve, START + p + 1)
                        pool.wait_ge(x1_done, (p + 1) * 2)
                        nc.gpsimd.tensor_tensor(
                            xr[:, 2 * i:2 * i + 2, :], xr[:, 2 * i:2 * i + 2, :],
                            biasw[:].unsqueeze(1).to_broadcast([P, 2, D]), ALU.add).then_inc(xbias_done, 1)

            def setup():
                pool.wait_ge(split_step, AHEAD["qk"] * SPLIT_STEPS)
                pool.wait_ge(dve_split, 2 * SPLIT_STEPS)
                stack_quarter(nc.gpsimd, 0, range(HQ - 1, HQ), [stacked_by_pool])
                pool.wait_ge(stacked_by_pool, STACK // HQ)

            sections(pool, part, setup)

        @block.scalar
        def _(act):
            def setup():
                act.wait_ge(split_step, AHEAD["qk"] * SPLIT_STEPS)
                act.wait_ge(dve_split, 2 * SPLIT_STEPS)
                act.wait_ge(setup_pe, 1)
                nc.scalar.copy(wo_T, ring[:, 0, 0, :].rearrange("p (a n) -> p a n", a=2)).then_inc(setup_act, 1)
                act.wait_ge(setup_pe, 2)
                nc.scalar.copy(wkv[:], ring[:, 1, :, :]).then_inc(setup_act, 1)
                act.wait_ge(setup_pe, 3)
                nc.scalar.copy(wop[:], ring[:, 2, 0, :].rearrange("p (a n) -> p a n", a=2)).then_inc(setup_act, 1)
                act.wait_ge(setup_pe, 4)
                nc.scalar.copy(wow[:, :, D:2 * D],
                               ring[:, 0, 0, :].rearrange("p (a n) -> p a n", a=2)).then_inc(setup_act, 1)

            def part(steps, p, linear):
                slot, rank = slots_of(steps), ranks(steps)
                for step in steps:
                    kind, i, r = step[0], index(step), rank[step]
                    if kind in filled and kind not in ("tile", "y", "T", "VK", "v"):
                        act.wait_ge(filled[kind], START + before(p, kind) + r + 1)
                        ps = ring[:, slot[step][0], :, :]
                    if kind == "tile":
                        g, c = i // HQ, i % HQ
                        act.wait_ge(max_ready, START + p * TILES + i + 1)
                        e = E[:, (g % EG) * HQ + c, :]
                        nc.scalar.activation(e, e, ACT.Exp, bias=negmax[:, i % NM:i % NM + 1], scale=-1.0,
                                             accum_out=sums[:, g % EG, c:c + 1]).then_inc(exp_done, 1)
                    elif kind == "u":
                        nc.scalar.activation(ps[:, 0, 0:D], ps[:, 0, 0:D], ACT.Square,
                                             accum_out=ssu[:, i:i + 1]).then_inc(u_act, 1)
                        act.wait_ge(w_dve, p * NT + i + 1)
                        nc.scalar.activation(ps[:, 1, 0:D], ps[:, 1, 0:D], ACT.Square,
                                             accum_out=ssw[:, i:i + 1]).then_inc(w_sq, 1)
                    elif kind == "gelu":
                        act.wait_ge(norm_step, (p + 1) * 5)
                        for t in range(NT):
                            nc.scalar.activation(wb[:, t, 0:D], wb[:, t, 0:D], ACT.Gelu,
                                                 scale=gsc[:, t:t + 1]).then_inc(gelu_done, 1)
                    elif kind == "xt":
                        act.wait_ge(filled["qk"], START + (p + 1) * PER["qk"])
                        act.wait_ge(filled["v"], START + (p + 1) * PER["v"])
                        nc.scalar.copy(XT[:, i, :].rearrange("p (b n) -> p b n", b=NB), ps).then_inc(xt_act, 1)
                    elif kind == "xt2":
                        act.wait_ge(filled["xt"], START + (p + 2) * DC)
                        nc.scalar.copy(XT2[:, i, :].rearrange("p (b n) -> p b n", b=NB), ps).then_inc(xt2_act, 1)
                    elif kind == "qk":
                        if steps is not prologue:
                            act.wait_ge(split_step, (before(p, "qk") + r - 1) * SPLIT_STEPS)
                        elif i == 2:
                            act.wait_ge(split_step, 3 * SPLIT_STEPS)
                        elif i == 3:
                            act.wait_ge(dve_split, SPLIT_STEPS)
                        nc.scalar.activation(qstage[:, r % 2, :], ps[:, 0, :], ACT.Copy,
                                             scale=SCORE_SCALE if (i // 2) % 2 else 1.0).then_inc(qk_act, 1)
                    elif kind == "gram":
                        act.wait_ge(filled["G"], START + p)
                        nc.scalar.copy(S[:, i, :], ps[:, 0, 0:D + 1]).then_inc(gram_act, 1)
                    elif kind == "G":
                        nc.scalar.copy(G[:], ps[:, 0, :].rearrange("p (a n) -> p a n", a=2)).then_inc(G_act, 1)
                    elif kind == "H":
                        act.wait_ge(filled["y"], START + p * PER["y"])
                        nc.scalar.copy(H[:], ps[:, 0, :].rearrange("p (a n) -> p a n", a=2)).then_inc(H_act, 1)

            sections(act, part, setup)

        @block.vector
        def _(dve):
            def setup():
                dve.wait_ge(const_ready, 7)
                nc.vector.tensor_reduce(mask[:], ident[:].rearrange("p (k j) -> p j k", j=AH),
                                        axis=AX.X, op=ALU.add).then_inc(const_dve, 1)
                nc.vector.memset(zT[:], 0.0).then_inc(const_dve, 1)
                nc.vector.memset(sums[:, EG - 1, :], 1.0).then_inc(const_dve, 1)
                nc.vector.memset(wb[:, :, D:D + 1], 1.0).then_inc(const_dve, 1)
                dve.wait_ge(w_loaded, 9 * 16)
                for ec in range(DC):
                    nc.vector.tensor_copy(wo_perm[:, ec, :].rearrange("p (d h) -> p d h", h=AH),
                                          wo_rows[:, ec, :].rearrange("p (h d) -> p d h", h=AH)
                                          ).then_inc(const_dve, 1)
                nc.vector.tensor_scalar(nbk[:], brow[:, 0:D], float(N), None,
                                        ALU.mult).then_inc(const_dve, 1)
                nc.vector.tensor_copy(bqb[:], bqc[:].unsqueeze(2).to_broadcast([P, DC, P])).then_inc(const_dve, 1)

            def part(steps, p, linear):
                slot, rank = slots_of(steps), ranks(steps)
                for step in steps:
                    kind, i, r = step[0], index(step), rank[step]
                    if kind in ("tile", "u", "T", "VK", "H", "y", "v"):
                        dve.wait_ge(filled[kind], START + before(p, kind) + r + 1)
                        ps = ring[:, slot[step][0], :, :]
                    if kind == "tile":
                        g, c = i // HQ, i % HQ
                        if c == 0:
                            dve.wait_ge(av_done, av_count(p, g - EG))
                        nc.vector.tensor_scalar(
                            E[:, (g % EG) * HQ + c, :].rearrange("p (b n) -> p b n", b=NB), ps, -1.0, None,
                            ALU.mult, ALU.min, accum_out=negmax[:, i % NM:i % NM + 1]).then_inc(max_ready, 1)
                    elif kind == "z":
                        if i == 1:
                            dve.wait_ge(av_done, av_count(p - 1, GROUPS - 1))
                            dve.wait_ge(filled["u"], START + p * NT)
                        else:
                            dve.wait_ge(av_done, av_count(p, GROUPS // 2 - 1))
                            dve.wait_ge(filled["u"], START + (p + 1) * NT)
                        nc.vector.tensor_copy(zT[:, i, :].rearrange("p (b n) -> p b n", b=NB), O[:]).then_inc(z_dve, 1)
                    elif kind == "recip":
                        dve.wait_ge(exp_done, START + p * TILES + HQ * r)
                        nc.vector.reciprocal(rsum[:, i % EG, :], sums[:, i % EG, :]).then_inc(rsum_ready, 1)
                    elif kind == "u":
                        dve.wait_ge(filled["xt2"], START + linear_before(p, linear) * DC)
                        nc.vector.tensor_copy(wb[:, i, 0:D], ps[:, 1, 0:D]).then_inc(w_dve, 1)
                    elif kind == "x1":
                        k = NT // 2
                        dve.wait_ge(xr_loaded, (p + 1) * 16)
                        dve.wait_ge(gelu_done, p * NT + (i + 1) * k)
                        nc.vector.scalar_tensor_tensor(
                            out=xr[:, i * k:(i + 1) * k, :], in0=wb[:, i * k:(i + 1) * k, 0:D], scalar=0.5,
                            in1=xr[:, i * k:(i + 1) * k, :], op0=ALU.mult, op1=ALU.add).then_inc(x1_done, 1)
                    elif kind == "qk":
                        if steps is prologue and i % 2 == 1:
                            dve.wait_ge(qk_act, START + i + 1)
                            split(dve, nc.vector, qstage[:, 1, :], resid[:, 1, :], i // 2, 1, dve_split,
                                  SPLIT_STEPS * (i // 2))
                    elif kind == "ln_stats":
                        dve.wait_ge(xp_loaded, (p + 2) * 16)
                        nc.vector.bn_stats(stats[:, i, :], xp[:, i, :]).then_inc(ln_stats, 1)
                    elif kind == "ln_aggr":
                        dve.wait_ge(ln_stats, (p + 2) * NT)
                        nc.vector.memset(sink[:], 0.0)
                        for t in range(NT):
                            nc.vector.bn_aggr(mv[:, t, :], stats[:, t, :]).then_inc(ln_aggr, 1)
                    elif kind == "ln_rstd":
                        dve.wait_ge(ln_aggr, (p + 2) * NT)
                        nc.vector.tensor_scalar(rstd[:], mv[:, :, 1], LN_EPS, None, ALU.add).then_inc(var_ready, 1)
                    elif kind == "xn":
                        dve.wait_ge(rstd_ready, p + 2)
                        nc.vector.tensor_scalar(xp[:, i, :], xp[:, i, :], mv[:, i, 0:1], rstd[:, i:i + 1],
                                                ALU.subtract, ALU.mult).then_inc(xn_ready, 1)
                    elif kind == "ln2_stats":
                        dve.wait_ge(x1_done, p * 2 + i // 4 + 1)
                        nc.vector.bn_stats(stats2[:, i, :], xr[:, i, :]).then_inc(ln2_stats, 1)
                    elif kind == "ln2_aggr":
                        dve.wait_ge(ln2_stats, (p + 1) * NT)
                        nc.vector.memset(sink[:], 0.0)
                        for t in range(NT):
                            nc.vector.bn_aggr(mv2[:, t, :], stats2[:, t, :]).then_inc(ln2_aggr, 1)
                    elif kind == "ln2_rstd":
                        dve.wait_ge(ln2_aggr, (p + 1) * NT)
                        nc.vector.tensor_scalar(rstd2[:], mv2[:, :, 1], LN_EPS, None, ALU.add).then_inc(var2_ready, 1)
                    elif kind == "u_norm":
                        dve.wait_ge(u_act, (p + 1) * NT)
                        nc.vector.tensor_scalar(ssu[:], ssu[:], NORM_EPS2, None, ALU.max).then_inc(u_floored, 1)
                    elif kind == "w_norm":
                        dve.wait_ge(norm_step, p * 5 + 3)
                        nc.vector.tensor_scalar(ssw[:], ssw[:], NORM_EPS2, None, ALU.max).then_inc(w_floored, 1)
                    elif kind == "xn2":
                        dve.wait_ge(rstd2_ready, p + 1)
                        nc.vector.tensor_scalar(wb[:, i, 0:D], xr[:, i, :], mv2[:, i, 0:1], rstd2[:, i:i + 1],
                                                ALU.subtract, ALU.mult).then_inc(xn2_ready, 1)
                    elif kind == "v":
                        if i == 3:
                            dve.wait_ge(vsc_ready, START + p * GROUPS + 1)
                        elif steps is not prologue:
                            dve.wait_ge(vsc_ready, START + p * GROUPS + 3 * QG + 2 * i + 1 + 2)
                        nc.vector.tensor_copy(vcur[:, 2 * i:2 * i + 2, :],
                                       ps[:, 0, :].rearrange("p (a n) -> p a n", a=2)).then_inc(v_dve, 1)
                    elif kind == "T":
                        dve.wait_ge(filled["H"], START + p)
                        for mc in range(DC):
                            nc.vector.scalar_tensor_tensor(
                                out=T[:, mc, :], in0=bkb[:], scalar=S[:, mc, D:D + 1],
                                in1=ps[:, 0, mc * D:(mc + 1) * D], op0=ALU.mult, op1=ALU.add).then_inc(T_dve, 1)
                        nc.vector.tensor_tensor(rrow[:], ps[0:1, 1, 0:D], nbk[:], ALU.add).then_inc(T_dve, 1)
                    elif kind == "VK":
                        for jc in range(DC):
                            nc.vector.tensor_tensor(
                                VK[:, jc, 0:D].rearrange("p (k j) -> p k j", j=AH),
                                ps[:, 0, jc * D:(jc + 1) * D].rearrange("p (k j) -> p k j", j=AH),
                                mask[:].unsqueeze(1).to_broadcast([P, D // AH, AH]),
                                ALU.mult).then_inc(VK_dve, 1)
                    elif kind == "H":
                        dve.wait_ge(xbias_done, START + p * 4)
                        nc.vector.tensor_tensor(biasw[:], ps[:, 1, 0:D], bob[:], ALU.add).then_inc(bias_dve, 1)
                    elif kind == "y":
                        dve.wait_ge(xbias_done, START + p * 4 + i + 1)
                        nc.vector.tensor_tensor(
                            xr[:, 2 * i:2 * i + 2, :], ps[:, 0, :].rearrange("p (a n) -> p a n", a=2),
                            xr[:, 2 * i:2 * i + 2, :], ALU.add).then_inc(y_dve, 1)

            sections(dve, part, setup)

        @block.tensor
        def _(pe):
            mm = nc.tensor.matmul
            pe.wait_ge(const_ready, 7)
            pe.wait_ge(wqkv_loaded, 3 * 16)

            def setup():
                pe.wait_ge(v_dve, START + before(0, "v"))
                pe.wait_ge(w_loaded, 9 * 16)
                for lc in range(DC):
                    for mc in range(DC):
                        last = nc.tensor.transpose(ring[:, 0, 0, mc * D + lc * P:mc * D + (lc + 1) * P],
                                                   wow[:, lc, mc * P:(mc + 1) * P], ident[:])
                last.then_inc(setup_pe, 1)
                for ic in range(2 * DC):
                    for dc in range(DC):
                        last = nc.tensor.transpose(ring[:, 1, dc, ic * P:(ic + 1) * P],
                                                   kv_rows[:, ic, dc * P:(dc + 1) * P], ident[:])
                last.then_inc(setup_pe, 1)
                pe.wait_ge(const_dve, 8)
                for ec in range(DC):
                    for jc in range(DC):
                        last = nc.tensor.transpose(ring[:, 2, 0, jc * D + ec * P:jc * D + (ec + 1) * P],
                                                   wo_perm[:, ec, jc * P:(jc + 1) * P], ident[:])
                last.then_inc(setup_pe, 1)
                pe.wait_ge(setup_act, 1)
                for lc in range(DC):
                    for mc in range(DC):
                        last = mm(ring[:, 0, 0, lc * D:(lc + 1) * D], wo_T[:, mc, lc * P:(lc + 1) * P],
                                  wff_sb[:, mc, :], start=(mc == 0), stop=(mc == DC - 1))
                last.then_inc(setup_pe, 1)
                pe.wait_ge(setup_act, 4)
                pe.wait_ge(exp_zeroed, 1)
                for c in range(HQ):
                    for n in range(NB):
                        mm(O[32 * c:32 * c + 32, n, :], vsc[1][:, 2, c, :], E[:, 2 * HQ + c, n * BANK:(n + 1) * BANK],
                           start=True, stop=False)
                pe.wait_ge(stacked_by_pool, STACK // HQ)

            def part(steps, p, linear):
                slot, rank = slots_of(steps), ranks(steps)
                for step in steps:
                    kind, i, r = step[0], index(step), rank[step]
                    if kind in PSUM_STEPS:
                        where, had = slot[step]
                        ps = ring[:, where, :, :]
                        if had is not None:
                            done = slot_done(p, rank, had)
                            for s in FREED[had[1] if had[0] == "last" else had[0]]:
                                pe.wait_ge(s, START + done * {T_dve: 3, VK_dve: 2}.get(s, 1))
                    if kind == "tile":
                        q, j, c = i // QT, (i % QT) // HQ, i % HQ
                        if i % QT == 0:
                            pe.wait_ge(stacked[q % 2], p * 2 * STACK + (q // 2 + 1) * STACK)
                        kq = stack[q % 2]
                        for n in range(NB):
                            last = mm(ps[:, n, :], kq[:, 0, c, j * P:(j + 1) * P],
                                      kq[:, 1, c, n * BANK:(n + 1) * BANK], start=True, stop=True)
                        last.then_inc(filled["tile"], 1)
                    elif kind == "av":
                        g, n = i, step[2]
                        q, j = g // QG, g % QG
                        half, a = q // 2, q % 2
                        if n == 0:
                            pe.wait_ge(vsc_ready, START + p * GROUPS + r)
                            if a == 0 and j == 0:
                                pe.wait_ge(z_dve, START + p * HALVES + half + 1)
                        for c in range(HQ):
                            last = mm(O[32 * c:32 * c + 32, n, :], vsc[a][:, g % EG, c, :],
                                      E[:, (g % EG) * HQ + c, n * BANK:(n + 1) * BANK],
                                      start=(a == 0 and j == 0), stop=(a == 1 and j == QG - 1))
                        if n == NB - 1:
                            last.then_inc(av_done, 1)
                    elif kind == "u":
                        pe.wait_ge(z_dve, START + p * HALVES + 1)
                        for n in range(2):
                            for h in range(HALVES):
                                last = mm(ps[:, n, 0:D], zT[:, h, i * P:(i + 1) * P],
                                          wow[:, h, n * D:(n + 1) * D],
                                          start=(h == 0), stop=(h == HALVES - 1))
                        last.then_inc(filled["u"], 1)
                    elif kind in ("xt", "xt2"):
                        src = xp if kind == "xt" else wb
                        if kind == "xt":
                            pe.wait_ge(xn_ready, (p + 2) * NT)
                        else:
                            pe.wait_ge(xn2_ready, (p + 1) * NT)
                        for t in range(NT):
                            col = (t % 4) * P
                            last = nc.tensor.transpose(ps[:, t // 4, col:col + P],
                                                       src[:, t, i * P:(i + 1) * P], ident[:])
                        last.then_inc(filled[kind], 1)
                    elif kind == "qk":
                        half, m, n = i // 4, (i // 2) % 2, i % 2
                        col = (D if m == 0 else 0) + half * P
                        pe.wait_ge(xt_act, START + (p + (1 if half else 2)) * DC)
                        for dc in range(DC):
                            last = mm(ps[:, 0, :], wqkv[:, dc, col:col + P],
                                      XT[:, dc, n * BANK:(n + 1) * BANK], start=(dc == 0), stop=(dc == DC - 1))
                        last.then_inc(filled["qk"], 1)
                    elif kind == "v":
                        pe.wait_ge(xt_act, START + (p + (1 if i == 3 else 2)) * DC)
                        for k in range(2):
                            t = 2 * i + k
                            for dc in range(DC):
                                last = mm(ps[:, 0, k * D:(k + 1) * D], XT[:, dc, t * P:(t + 1) * P],
                                          wqkv[:, dc, 2 * D:3 * D], start=(dc == 0), stop=(dc == DC - 1))
                        last.then_inc(filled["v"], 1)
                    elif kind == "gram":
                        pe.wait_ge(xn2_ready, (p + 1) * NT)
                        for t in range(NT):
                            last = mm(ps[:, 0, i * P:D + 1], wb[:, t, i * P:(i + 1) * P], wb[:, t, i * P:],
                                      start=(t == 0), stop=(t == NT - 1))
                        if i == 1:
                            pe.wait_ge(gram_act, START + p * DC + 1)
                            last = nc.tensor.transpose(ps[:, 0, 0:P], S[:, 0, P:D], ident[:])
                        last.then_inc(filled["gram"], 1)
                    elif kind == "T":
                        pe.wait_ge(gram_act, START + (p + 1) * DC)
                        for mc in range(DC):
                            for kc in range(DC):
                                mm(ps[:, 0, mc * D:(mc + 1) * D], S[:, kc, mc * P:(mc + 1) * P],
                                   wkv[:, kc, 0:D], start=(kc == 0), stop=(kc == DC - 1))
                        for kc in range(DC):
                            last = mm(ps[0:1, 1, 0:D], S[:, kc, D:D + 1], wkv[:, kc, 0:D],
                                      start=(kc == 0), stop=(kc == DC - 1))
                        last.then_inc(filled["T"], 1)
                    elif kind == "VK":
                        pe.wait_ge(T_dve, START + (p + 1) * 3)
                        for jc in range(DC):
                            o = ps[:, 0, jc * D:(jc + 1) * D]
                            for dc in range(DC):
                                mm(o, wkv[:, dc, D + jc * P:D + (jc + 1) * P], T[:, dc, :],
                                   start=(dc == 0), stop=False)
                            last = mm(o, brow[0:1, D + jc * P:D + (jc + 1) * P], rrow[:],
                                      start=False, stop=True)
                        last.then_inc(filled["VK"], 1)
                    elif kind == "G":
                        pe.wait_ge(VK_dve, START + (p + 1) * 2)
                        for ic in range(DC):
                            for jc in range(DC):
                                last = mm(ps[:, 0, ic * D:(ic + 1) * D], VK[:, jc, ic * P:(ic + 1) * P],
                                          wop[:, jc, :], start=(jc == 0), stop=(jc == DC - 1))
                        last.then_inc(filled["G"], 1)
                    elif kind == "H":
                        pe.wait_ge(G_act, START + p + 1)
                        for dc in range(DC):
                            for ic in range(DC):
                                mm(ps[:, 0, dc * D:(dc + 1) * D], wqn[:, ic, dc * P:(dc + 1) * P],
                                   G[:, ic, :], start=(ic == 0), stop=(ic == DC - 1))
                        for ic in range(DC):
                            last = mm(ps[:, 1, 0:D], bqb[:, ic, :], G[:, ic, :],
                                      start=(ic == 0), stop=(ic == DC - 1))
                        last.then_inc(filled["H"], 1)
                    elif kind == "y":
                        pe.wait_ge(H_act, START + p + 1)
                        pe.wait_ge(xt2_act, START + (p + 1) * DC)
                        for k in range(2):
                            t = 2 * i + k
                            for dc in range(DC):
                                last = mm(ps[:, 0, k * D:(k + 1) * D], XT2[:, dc, t * P:(t + 1) * P],
                                          H[:, dc, :], start=(dc == 0), stop=(dc == DC - 1))
                        last.then_inc(filled["y"], 1)

            sections(pe, part, setup)


_INS = ['L0_attn_x', 'L0_attn_w_qkv', 'L0_attn_b_qkv', 'L0_attn_w_o', 'L0_attn_b_o', 'L0_ffn_Wq',
        'L0_ffn_Wk', 'L0_ffn_Wv', 'L0_ffn_Wo', 'L0_ffn_Wff']
_OUTS = [((8, 1024, 256), 'float32')]


def kernel(**inputs):
    import numpy as _np
    import concourse.bacc as _bacc
    from concourse import mybir as _mybir
    from concourse.bass_utils import run_bass_kernel_spmd as _run

    nc = _bacc.Bacc("TRN2", target_bir_lowering=False, num_devices=1)
    arrays, args = {}, []
    for name in _INS:
        a = _np.ascontiguousarray(inputs[name])
        arrays[f"in_{name}"] = a
        args.append(nc.dram_tensor(f"in_{name}", a.shape, _mybir.dt.from_np(a.dtype), kind="ExternalInput").ap())
    for i, (shape, dtype) in enumerate(_OUTS):
        dt = _mybir.dt.from_np(_np.dtype(dtype))
        args.append(nc.dram_tensor(f"out_{i}", shape, dt, kind="ExternalOutput").ap())
    build_macaron(nc, *args)
    r = _run(nc, [arrays], core_ids=[0])
    return r.results[0]["out_0"]
```
